# Optimizing a Trainium2 kernel written in Bass

```python
import numpy as np
import jax
import jax.numpy as jnp

def _softmax(x, axis=-1):
    return jax.nn.softmax(x, axis=axis)

def _gelu(x):
    return jax.nn.gelu(x, approximate=True)

def _silu(x):
    return jax.nn.silu(x)

def _sigmoid(x):
    return jax.nn.sigmoid(x)

def _layernorm(x, axis=-1, eps=1e-05):
    m = jnp.mean(x, axis=axis, keepdims=True)
    v = jnp.var(x, axis=axis, keepdims=True)
    return (x - m) / jnp.sqrt(v + eps)

def _scatter_add(tgt, idx, src, axis=0):
    return tgt.at[idx].add(src)

def _segment_sum(src, seg, n):
    return jax.ops.segment_sum(src, seg, n)
kernel_name = 'mk_xattn_ffn_d4_seqx_r4_d07c09'

def setup_inputs(seed: int=0):
    np.random.seed(seed)
    _w = jnp.asarray

    def _rec_inputs():
        import jax
        import jax.numpy as jnp
        _rk = jax.random.key(seed)
        x = -0.0003929 + 0.9999 * jax.random.normal(jax.random.fold_in(_rk, 1), (8, 256, 512), jnp.float32)
        _lenS = 256 - jax.random.randint(jax.random.fold_in(_rk, 7), (8,), 0, max(1, 256 // 4) + 1, jnp.int32)
        _lenS2 = 256 - jax.random.randint(jax.random.fold_in(_rk, 8), (8,), 0, max(1, 256 // 4) + 1, jnp.int32)
        _ctx_1024P = jax.random.normal(jax.random.fold_in(_rk, 11), (8, 16, 256), jnp.float32)
        _ctx_1024c = jax.random.dirichlet(jax.random.fold_in(_rk, 511), 0.3 * jnp.ones((16,), jnp.float32), (8, 256))
        _ctx_1024t = jnp.einsum('bsk,bkd->bsd', _ctx_1024c, _ctx_1024P)
        _ctx_1024t = _ctx_1024t * jax.lax.rsqrt(jnp.mean(jnp.square(_ctx_1024t)) + 1e-12) * 0.953939
        ctx_1024 = -0.000494167 + 1.00018 * (_ctx_1024t + 0.3 * jax.random.normal(jax.random.fold_in(_rk, 611), (8, 256, 256), jnp.float32))
        fside_BxSx2_0 = jax.random.uniform(jax.random.fold_in(_rk, 13), (8, 256, 2), jnp.float32, 0.0, 0.999707)
        _validS = jnp.arange(256)[None, :] < _lenS[:, None]
        _validS2 = jnp.arange(256)[None, :] < _lenS2[:, None]
        _causal = jnp.tril(jnp.ones((256, 256), dtype=bool))
        mask_BxS2_bf1 = jnp.ones((8, 256), dtype=bool)
        return (x, ctx_1024, fside_BxSx2_0, mask_BxS2_bf1)
    x, ctx_1024, fside_BxSx2_0, mask_BxS2_bf1 = _rec_inputs()

    def _L0_xattn_setup():
        import jax, jax.numpy as jnp
        import numpy as np
        N_HEADS = 16
        N_KV_HEADS = 8
        HEAD_DIM = 128
        D_TEXT = 512
        D_VISION = 256
        GROUPS = N_HEADS // N_KV_HEADS
        key = jax.random.key(seed)
        ks = jax.random.split(key, 6)
        B, T_text, T_vis = (4, 512, 144)
        text_hidden = jax.random.normal(ks[0], (B, T_text, D_TEXT), dtype=jnp.float32)
        vision_tokens = jax.random.normal(ks[1], (B, T_vis, D_VISION), dtype=jnp.float32)
        vision_mask = jnp.ones((B, T_vis), dtype=bool)
        s = 0.02
        Wq = jax.random.normal(ks[2], (D_TEXT, N_HEADS * HEAD_DIM), dtype=jnp.float32) * s
        Wk = jax.random.normal(ks[3], (D_VISION, N_KV_HEADS * HEAD_DIM), dtype=jnp.float32) * s
        Wv = jax.random.normal(ks[4], (D_VISION, N_KV_HEADS * HEAD_DIM), dtype=jnp.float32) * s
        Wo = jax.random.normal(ks[5], (N_HEADS * HEAD_DIM, D_TEXT), dtype=jnp.float32) * s
        return {'text_hidden': text_hidden, 'vision_tokens': vision_tokens, 'vision_mask': vision_mask, 'Wq': Wq, 'Wk': Wk, 'Wv': Wv, 'Wo': Wo}
    _L0_xattn_all = _L0_xattn_setup()
    _L0_xattn_in = {k: v for k, v in _L0_xattn_all.items() if k in ('Wq', 'Wk', 'Wv', 'Wo')}
    del _L0_xattn_all

    def _L0_ffn_setup():
        import jax, jax.numpy as jnp
        import numpy as np
        TOP_K = 2
        key = jax.random.key(seed)
        ks = jax.random.split(key, 4)
        G, S, F, E, H = (4, 512, 512, 8, 512)
        return {'x': jax.random.normal(ks[0], (G, S, F), dtype=jnp.float32), 'router_logits': jax.random.normal(ks[1], (F, E), dtype=jnp.float32) * 0.02, 'gating_einsum': jax.random.normal(ks[2], (E, 2, H, F), dtype=jnp.float32) * 0.02, 'linear': jax.random.normal(ks[3], (E, H, F), dtype=jnp.float32) * 0.02, 'per_expert_scale': jnp.ones((E,), dtype=jnp.float32), 'router_scale': jnp.ones((F,), dtype=jnp.float32)}
    _L0_ffn_all = _L0_ffn_setup()
    _L0_ffn_in = {k: v for k, v in _L0_ffn_all.items() if k in ('router_logits', 'gating_einsum', 'linear', 'per_expert_scale', 'router_scale')}
    del _L0_ffn_all

    def _L1_xattn_setup():
        import jax, jax.numpy as jnp
        import numpy as np
        B, S1, S2, DCA = (2, 512, 256, 16)
        QDIM, KDIM, H = (512, 256, 16)
        HD = QDIM // H
        SCALE = HD ** (-0.5)
        EPS = 1e-06
        DCA_WEIGHT = 1.0

        def _ln(t, w, b):
            m = jnp.mean(t, axis=-1, keepdims=True)
            v = jnp.var(t, axis=-1, keepdims=True)
            return (t - m) * jax.lax.rsqrt(v + EPS) * w + b

        def _attn(q, k, v):
            s = jnp.einsum('bhqd,bhkd->bhqk', q, k) * SCALE
            p = jax.nn.softmax(s, axis=-1)
            return jnp.einsum('bhqk,bhkd->bhqd', p, v)
        key = jax.random.key(seed)
        ks = jax.random.split(key, 8)
        w = lambda k, shape: jax.random.normal(k, shape, jnp.float32) * 0.02
        return {'x': jax.random.normal(ks[0], (B, S1, QDIM), jnp.float32), 'y': jax.random.normal(ks[1], (B, S2 + DCA, KDIM), jnp.float32), 'Wq': w(ks[2], (QDIM, QDIM)), 'bq': jnp.zeros((QDIM,), jnp.float32), 'Wk': w(ks[3], (KDIM, QDIM)), 'bk': jnp.zeros((QDIM,), jnp.float32), 'Wv': w(ks[4], (KDIM, QDIM)), 'bv': jnp.zeros((QDIM,), jnp.float32), 'Wkv_dca': w(ks[5], (KDIM, 2 * QDIM)), 'bkv_dca': jnp.zeros((2 * QDIM,), jnp.float32), 'qn_w': jnp.ones((HD,), jnp.float32), 'qn_b': jnp.zeros((HD,), jnp.float32), 'kn_w': jnp.ones((HD,), jnp.float32), 'kn_b': jnp.zeros((HD,), jnp.float32), 'kn_dca_w': jnp.ones((HD,), jnp.float32), 'kn_dca_b': jnp.zeros((HD,), jnp.float32), 'Wo': w(ks[6], (QDIM, QDIM)), 'bo': jnp.zeros((QDIM,), jnp.float32)}
    _L1_xattn_all = _L1_xattn_setup()
    _L1_xattn_in = {k: v for k, v in _L1_xattn_all.items() if k in ('Wq', 'bq', 'Wk', 'bk', 'Wv', 'bv', 'Wkv_dca', 'bkv_dca', 'qn_w', 'qn_b', 'kn_w', 'kn_b', 'kn_dca_w', 'kn_dca_b', 'Wo', 'bo')}
    del _L1_xattn_all

    def _L1_ffn_setup():
        import jax, jax.numpy as jnp
        import numpy as np
        D_MODEL = 512
        D_EXPERT = 2048
        EPS = 1e-08

        def ternary_quant(w):
            scale = jnp.mean(jnp.abs(w)) + EPS
            q = jnp.clip(jnp.round(w / scale), -1.0, 1.0) * scale
            return w + jax.lax.stop_gradient(q - w)
        key = jax.random.key(seed)
        k_x, k_up, k_gate, k_down = jax.random.split(key, 4)
        std_in = 1.0 / np.sqrt(D_MODEL)
        std_exp = 1.0 / np.sqrt(D_EXPERT)
        return {'x': jax.random.normal(k_x, (4, 512, D_MODEL), dtype=jnp.float32), 'W_up': jax.random.normal(k_up, (D_EXPERT, D_MODEL), dtype=jnp.float32) * std_in, 'W_gate': jax.random.normal(k_gate, (D_EXPERT, D_MODEL), dtype=jnp.float32) * std_in, 'W_down': jax.random.normal(k_down, (D_MODEL, D_EXPERT), dtype=jnp.float32) * std_exp}
    _L1_ffn_all = _L1_ffn_setup()
    _L1_ffn_in = {k: v for k, v in _L1_ffn_all.items() if k in ('W_up', 'W_gate', 'W_down')}
    del _L1_ffn_all

    def _L2_xattn_setup():
        import jax, jax.numpy as jnp
        import numpy as np
        DIM = 512
        CTX_DIM = 256
        N_HEADS = 32
        HEAD_DIM = DIM // N_HEADS
        POS_DIM = 2
        B, N, CTXN = (2, 512, 512)
        ROPE_BASE = 10000.0

        def apply_axial_rope(x, pos):
            b, n, h, d = x.shape
            p = pos.shape[-1]
            dpa = d // p
            half = dpa // 2
            freqs = ROPE_BASE ** (-jnp.arange(half, dtype=x.dtype) / half)
            ang = pos[..., :, None] * freqs
            cos = jnp.cos(ang)[:, :, None, :, :]
            sin = jnp.sin(ang)[:, :, None, :, :]
            xr = x.reshape(b, n, h, p, half, 2)
            x1, x2 = (xr[..., 0], xr[..., 1])
            out = jnp.stack([x1 * cos - x2 * sin, x1 * sin + x2 * cos], axis=-1)
            return out.reshape(b, n, h, d)
        key = jax.random.key(seed)
        ks = jax.random.split(key, 8)
        x = jax.random.normal(ks[0], (B, N, DIM), jnp.float32)
        ctx = jax.random.normal(ks[1], (B, CTXN, CTX_DIM), jnp.float32)
        pos_map = jax.random.uniform(ks[2], (B, N, POS_DIM), jnp.float32)
        ctx_pos_map = jax.random.uniform(ks[3], (B, CTXN, POS_DIM), jnp.float32)
        Wq = jax.random.normal(ks[4], (DIM, DIM), jnp.float32) / np.sqrt(DIM)
        Wkv = jax.random.normal(ks[5], (CTX_DIM, 2 * DIM), jnp.float32) / np.sqrt(CTX_DIM)
        Wout = jax.random.normal(ks[6], (DIM, DIM), jnp.float32) / np.sqrt(DIM)
        bout = jnp.zeros((DIM,), jnp.float32)
        return {'x': x, 'ctx': ctx, 'pos_map': pos_map, 'ctx_pos_map': ctx_pos_map, 'Wq': Wq, 'Wkv': Wkv, 'Wout': Wout, 'bout': bout}
    _L2_xattn_all = _L2_xattn_setup()
    _L2_xattn_in = {k: v for k, v in _L2_xattn_all.items() if k in ('Wq', 'Wkv', 'Wout', 'bout')}
    del _L2_xattn_all

    def _L2_ffn_setup():
        import math
        import jax, jax.numpy as jnp
        import numpy as np
        DIM = 512
        RANK = 8
        B, T = (4, 1024)

        def _orthogonal(key, n):
            a = jax.random.normal(key, (n, n), dtype=jnp.float32)
            q, r = jnp.linalg.qr(a)
            q = q * jnp.sign(jnp.diagonal(r))[None, :]
            return q
        key = jax.random.key(seed)
        kx, kf = jax.random.split(key)
        x = jax.random.normal(kx, (B, T, DIM), dtype=jnp.float32)
        fkeys = jax.random.split(kf, RANK)
        factors = jnp.stack([_orthogonal(fkeys[r], DIM) * (r + 1) ** (-0.5) for r in range(RANK)])
        bias = jnp.zeros((DIM,), dtype=jnp.float32)
        return {'x': x, 'factors': factors, 'bias': bias}
    _L2_ffn_all = _L2_ffn_setup()
    _L2_ffn_in = {k: v for k, v in _L2_ffn_all.items() if k in ('factors', 'bias')}
    del _L2_ffn_all

    def _L3_xattn_setup():
        import jax, jax.numpy as jnp
        import numpy as np
        EPS = 1e-05

        def rmsnorm(x, g, eps=EPS):
            var = jnp.mean(jnp.square(x), axis=-1, keepdims=True)
            return x * jax.lax.rsqrt(var + eps) * g
        key = jax.random.key(seed)
        ks = jax.random.split(key, 8)
        B, Sq, Skv = (2, 1024, 128)
        dim, cdim, H, D = (512, 256, 16, 128)
        inner = H * D
        s = lambda f: 1.0 / np.sqrt(f)
        return {'hidden_states': jax.random.normal(ks[0], (B, Sq, dim), jnp.float32), 'encoder_hidden_states': jax.random.normal(ks[1], (B, Skv, cdim), jnp.float32), 'Wq': jax.random.normal(ks[2], (dim, inner), jnp.float32) * s(dim), 'Wk': jax.random.normal(ks[3], (cdim, inner), jnp.float32) * s(cdim), 'Wv': jax.random.normal(ks[4], (cdim, inner), jnp.float32) * s(cdim), 'Wo': jax.random.normal(ks[5], (inner, dim), jnp.float32) * s(inner), 'gq': jnp.ones((D,), jnp.float32), 'gk': jnp.ones((D,), jnp.float32)}
    _L3_xattn_all = _L3_xattn_setup()
    _L3_xattn_in = {k: v for k, v in _L3_xattn_all.items() if k in ('Wq', 'Wk', 'Wv', 'Wo', 'gq', 'gk')}
    del _L3_xattn_all

    def _L3_ffn_setup():
        import jax, jax.numpy as jnp
        import numpy as np
        NUM_EXPERTS = 16
        C = 1.0
        key = jax.random.key(seed)
        k1, k2, k3 = jax.random.split(key, 3)
        b, s, h = (4, 512, 512)
        return {'x': jax.random.normal(k1, (b, s, h), dtype=jnp.float32), 'router_w': jax.random.normal(k2, (h, NUM_EXPERTS), dtype=jnp.float32) * 0.02, 'router_b': jnp.zeros((NUM_EXPERTS,), dtype=jnp.float32), 'expert_w': jax.random.normal(k3, (h, h), dtype=jnp.float32) * 0.02, 'expert_b': jnp.zeros((h,), dtype=jnp.float32)}
    _L3_ffn_all = _L3_ffn_setup()
    _L3_ffn_in = {k: v for k, v in _L3_ffn_all.items() if k in ('router_w', 'router_b', 'expert_w', 'expert_b')}
    del _L3_ffn_all
    return {'x': x, 'ctx_1024': ctx_1024, 'fside_BxSx2_0': fside_BxSx2_0, 'mask_BxS2_bf1': mask_BxS2_bf1, 'L0_xattn_Wq': _L0_xattn_in['Wq'], 'L0_xattn_Wk': _L0_xattn_in['Wk'], 'L0_xattn_Wv': _L0_xattn_in['Wv'], 'L0_xattn_Wo': _L0_xattn_in['Wo'], 'L0_ffn_router_logits': _L0_ffn_in['router_logits'], 'L0_ffn_gating_einsum': _L0_ffn_in['gating_einsum'], 'L0_ffn_linear': _L0_ffn_in['linear'], 'L0_ffn_per_expert_scale': _L0_ffn_in['per_expert_scale'], 'L0_ffn_router_scale': _L0_ffn_in['router_scale'], 'L1_xattn_Wq': _L1_xattn_in['Wq'], 'L1_xattn_bq': _L1_xattn_in['bq'], 'L1_xattn_Wk': _L1_xattn_in['Wk'], 'L1_xattn_bk': _L1_xattn_in['bk'], 'L1_xattn_Wv': _L1_xattn_in['Wv'], 'L1_xattn_bv': _L1_xattn_in['bv'], 'L1_xattn_Wkv_dca': _L1_xattn_in['Wkv_dca'], 'L1_xattn_bkv_dca': _L1_xattn_in['bkv_dca'], 'L1_xattn_qn_w': _L1_xattn_in['qn_w'], 'L1_xattn_qn_b': _L1_xattn_in['qn_b'], 'L1_xattn_kn_w': _L1_xattn_in['kn_w'], 'L1_xattn_kn_b': _L1_xattn_in['kn_b'], 'L1_xattn_kn_dca_w': _L1_xattn_in['kn_dca_w'], 'L1_xattn_kn_dca_b': _L1_xattn_in['kn_dca_b'], 'L1_xattn_Wo': _L1_xattn_in['Wo'], 'L1_xattn_bo': _L1_xattn_in['bo'], 'L1_ffn_W_up': _L1_ffn_in['W_up'], 'L1_ffn_W_gate': _L1_ffn_in['W_gate'], 'L1_ffn_W_down': _L1_ffn_in['W_down'], 'L2_xattn_Wq': _L2_xattn_in['Wq'], 'L2_xattn_Wkv': _L2_xattn_in['Wkv'], 'L2_xattn_Wout': _L2_xattn_in['Wout'], 'L2_xattn_bout': _L2_xattn_in['bout'], 'L2_ffn_factors': _L2_ffn_in['factors'], 'L2_ffn_bias': _L2_ffn_in['bias'], 'L3_xattn_Wq': _L3_xattn_in['Wq'], 'L3_xattn_Wk': _L3_xattn_in['Wk'], 'L3_xattn_Wv': _L3_xattn_in['Wv'], 'L3_xattn_Wo': _L3_xattn_in['Wo'], 'L3_xattn_gq': _L3_xattn_in['gq'], 'L3_xattn_gk': _L3_xattn_in['gk'], 'L3_ffn_router_w': _L3_ffn_in['router_w'], 'L3_ffn_router_b': _L3_ffn_in['router_b'], 'L3_ffn_expert_w': _L3_ffn_in['expert_w'], 'L3_ffn_expert_b': _L3_ffn_in['expert_b']}

def reference(x, ctx_1024, fside_BxSx2_0, mask_BxS2_bf1, L0_xattn_Wq, L0_xattn_Wk, L0_xattn_Wv, L0_xattn_Wo, L0_ffn_router_logits, L0_ffn_gating_einsum, L0_ffn_linear, L0_ffn_per_expert_scale, L0_ffn_router_scale, L1_xattn_Wq, L1_xattn_bq, L1_xattn_Wk, L1_xattn_bk, L1_xattn_Wv, L1_xattn_bv, L1_xattn_Wkv_dca, L1_xattn_bkv_dca, L1_xattn_qn_w, L1_xattn_qn_b, L1_xattn_kn_w, L1_xattn_kn_b, L1_xattn_kn_dca_w, L1_xattn_kn_dca_b, L1_xattn_Wo, L1_xattn_bo, L1_ffn_W_up, L1_ffn_W_gate, L1_ffn_W_down, L2_xattn_Wq, L2_xattn_Wkv, L2_xattn_Wout, L2_xattn_bout, L2_ffn_factors, L2_ffn_bias, L3_xattn_Wq, L3_xattn_Wk, L3_xattn_Wv, L3_xattn_Wo, L3_xattn_gq, L3_xattn_gk, L3_ffn_router_w, L3_ffn_router_b, L3_ffn_expert_w, L3_ffn_expert_b):
    import jax
    import jax.numpy as jnp

    def _L0_xattn_ref(text_hidden, vision_tokens, vision_mask, Wq, Wk, Wv, Wo):
        import jax, jax.numpy as jnp
        import numpy as np
        N_HEADS = 16
        N_KV_HEADS = 8
        HEAD_DIM = 128
        D_TEXT = 512
        D_VISION = 256
        GROUPS = N_HEADS // N_KV_HEADS
        B, T_text, _ = text_hidden.shape
        T_vis = vision_tokens.shape[1]
        scale = jnp.float32(np.sqrt(HEAD_DIM))
        q = (text_hidden @ Wq).reshape(B, T_text, N_HEADS, HEAD_DIM).transpose(0, 2, 1, 3)
        k = (vision_tokens @ Wk).reshape(B, T_vis, N_KV_HEADS, HEAD_DIM).transpose(0, 2, 1, 3)
        v = (vision_tokens @ Wv).reshape(B, T_vis, N_KV_HEADS, HEAD_DIM).transpose(0, 2, 1, 3)
        k = jnp.repeat(k, GROUPS, axis=1)
        v = jnp.repeat(v, GROUPS, axis=1)
        scores = jnp.einsum('bhtd,bhsd->bhts', q, k) / scale
        mask = vision_mask[:, None, None, :]
        scores = jnp.where(mask, scores, -jnp.inf)
        attn = jax.nn.softmax(scores, axis=-1)
        attn = jnp.nan_to_num(attn, nan=0.0)
        out = jnp.einsum('bhts,bhsd->bhtd', attn, v)
        out = out.transpose(0, 2, 1, 3).reshape(B, T_text, N_HEADS * HEAD_DIM)
        return out @ Wo

    def _L0_ffn_ref(x, router_logits, gating_einsum, linear, per_expert_scale, router_scale):
        import jax, jax.numpy as jnp
        import numpy as np
        TOP_K = 2
        G, S, F = x.shape
        E = router_logits.shape[-1]
        H = linear.shape[1]
        k = TOP_K
        dtype = x.dtype
        var = jnp.mean(jnp.square(x.astype(jnp.float32)), axis=-1, keepdims=True)
        router_input = x * jax.lax.rsqrt(var + 1e-06).astype(dtype)
        root_size = jax.lax.rsqrt(jnp.array(F, dtype=dtype))
        router_input = router_input * root_size * router_scale.astype(dtype)
        logits = jnp.einsum('gsd,de->gse', router_input, router_logits.astype(dtype))
        logits32 = logits.astype(jnp.float32)
        probs = jax.nn.softmax(logits32, axis=-1)
        _, choices = jax.lax.approx_max_k(logits32, k=k)
        indicator = jax.nn.one_hot(choices, E, dtype=probs.dtype).sum(axis=-2)
        renorm = jnp.sum(indicator * probs, axis=-1, keepdims=True)
        renorm = jnp.where(renorm > 0.0, renorm, 1.0)
        weights = probs / renorm
        x_flat = x.reshape((-1, F))
        batch_size = G * S
        choices_flat = choices.ravel()
        xs_order = choices_flat.argsort()
        xs_reverse_argsort = xs_order.argsort()
        xs_indices = jnp.repeat(jnp.arange(batch_size), k)[xs_order]
        sorted_xs = x_flat[xs_indices, :]
        choices_oh = jax.nn.one_hot(choices, num_classes=E, dtype=jnp.int32)
        tokens_per_expert = jnp.sum(choices_oh, axis=(0, 1, 2))
        combine_weights = (choices_oh.astype(jnp.float32) * jnp.expand_dims(weights, axis=2)).sum(axis=-1).astype(weights.dtype)
        w_gate = jnp.transpose(gating_einsum, (0, 3, 1, 2)).reshape(E, F, 2 * H)
        gate_out = jax.lax.ragged_dot(sorted_xs, w_gate.astype(dtype), group_sizes=tokens_per_expert)
        gate_out = gate_out.reshape(gate_out.shape[0], 2, H)
        activation = jax.nn.gelu(gate_out[:, 0, :]) * gate_out[:, 1, :]
        expert_outputs = jax.lax.ragged_dot(activation, linear.astype(dtype), group_sizes=tokens_per_expert)
        expert_indices = jnp.repeat(jnp.arange(E), tokens_per_expert, total_repeat_length=expert_outputs.shape[0])
        expert_outputs = expert_outputs * per_expert_scale.astype(expert_outputs.dtype)[expert_indices, None]
        out = expert_outputs[xs_reverse_argsort].reshape((G, S, k, -1))
        out = jnp.einsum('blkd,blk->bld', out, combine_weights, preferred_element_type=out.dtype)
        return out

    def _L1_xattn_ref(x, y, Wq, bq, Wk, bk, Wv, bv, Wkv_dca, bkv_dca, qn_w, qn_b, kn_w, kn_b, kn_dca_w, kn_dca_b, Wo, bo):
        import jax, jax.numpy as jnp
        import numpy as np
        B, S1, S2, DCA = (2, 512, 256, 16)
        QDIM, KDIM, H = (512, 256, 16)
        HD = QDIM // H
        SCALE = HD ** (-0.5)
        EPS = 1e-06
        DCA_WEIGHT = 1.0

        def _ln(t, w, b):
            m = jnp.mean(t, axis=-1, keepdims=True)
            v = jnp.var(t, axis=-1, keepdims=True)
            return (t - m) * jax.lax.rsqrt(v + EPS) * w + b

        def _attn(q, k, v):
            s = jnp.einsum('bhqd,bhkd->bhqk', q, k) * SCALE
            p = jax.nn.softmax(s, axis=-1)
            return jnp.einsum('bhqk,bhkd->bhqd', p, v)
        b, s1, _ = x.shape
        y_dca = y[:, -DCA:, :]
        y_main = y[:, :-DCA, :]
        kv_dca = (y_dca @ Wkv_dca + bkv_dca).reshape(b, DCA, 2, H, HD)
        k_dca = _ln(kv_dca[:, :, 0], kn_dca_w, kn_dca_b)
        v_dca = kv_dca[:, :, 1]
        s2 = y_main.shape[1]
        q = _ln((x @ Wq + bq).reshape(b, s1, H, HD), qn_w, qn_b)
        kv = jnp.concatenate([y_main @ Wk + bk, y_main @ Wv + bv], axis=-1)
        kv = kv.reshape(b, s2, H, 2 * HD)
        k = _ln(kv[..., :HD], kn_w, kn_b)
        v = kv[..., HD:]
        qT = q.transpose(0, 2, 1, 3)
        ctx = _attn(qT, k.transpose(0, 2, 1, 3), v.transpose(0, 2, 1, 3))
        ctx = ctx.transpose(0, 2, 1, 3).reshape(b, s1, QDIM)
        ctx_dca = _attn(qT, k_dca.transpose(0, 2, 1, 3), v_dca.transpose(0, 2, 1, 3))
        ctx_dca = ctx_dca.transpose(0, 2, 1, 3).reshape(b, s1, QDIM)
        ctx = ctx + DCA_WEIGHT * ctx_dca
        return ctx @ Wo + bo

    def _L1_ffn_ref(x, W_up, W_gate, W_down):
        import jax, jax.numpy as jnp
        import numpy as np
        D_MODEL = 512
        D_EXPERT = 2048
        EPS = 1e-08

        def ternary_quant(w):
            scale = jnp.mean(jnp.abs(w)) + EPS
            q = jnp.clip(jnp.round(w / scale), -1.0, 1.0) * scale
            return w + jax.lax.stop_gradient(q - w)
        wu = ternary_quant(W_up)
        wg = ternary_quant(W_gate)
        wd = ternary_quant(W_down)
        up = jnp.einsum('bsd,ed->bse', x, wu)
        gate = jnp.einsum('bsd,ed->bse', x, wg)
        hidden = jax.nn.silu(up) * gate
        return jnp.einsum('bse,de->bsd', hidden, wd)

    def _L2_xattn_ref(x, ctx, pos_map, ctx_pos_map, Wq, Wkv, Wout, bout):
        import jax, jax.numpy as jnp
        import numpy as np
        DIM = 512
        CTX_DIM = 256
        N_HEADS = 32
        HEAD_DIM = DIM // N_HEADS
        POS_DIM = 2
        B, N, CTXN = (2, 512, 512)
        ROPE_BASE = 10000.0

        def apply_axial_rope(x, pos):
            b, n, h, d = x.shape
            p = pos.shape[-1]
            dpa = d // p
            half = dpa // 2
            freqs = ROPE_BASE ** (-jnp.arange(half, dtype=x.dtype) / half)
            ang = pos[..., :, None] * freqs
            cos = jnp.cos(ang)[:, :, None, :, :]
            sin = jnp.sin(ang)[:, :, None, :, :]
            xr = x.reshape(b, n, h, p, half, 2)
            x1, x2 = (xr[..., 0], xr[..., 1])
            out = jnp.stack([x1 * cos - x2 * sin, x1 * sin + x2 * cos], axis=-1)
            return out.reshape(b, n, h, d)
        b, n, _ = x.shape
        ctx_n = ctx.shape[1]
        q = (x @ Wq).reshape(b, n, N_HEADS, HEAD_DIM)
        k, v = jnp.split(ctx @ Wkv, 2, axis=-1)
        k = k.reshape(b, ctx_n, N_HEADS, HEAD_DIM)
        v = v.reshape(b, ctx_n, N_HEADS, HEAD_DIM)
        q = apply_axial_rope(q, pos_map)
        k = apply_axial_rope(k, ctx_pos_map)
        scale = 1.0 / np.sqrt(HEAD_DIM).astype(np.float32)
        logits = jnp.einsum('bqhd,bkhd->bhqk', q, k) * scale
        w = jax.nn.softmax(logits, axis=-1)
        attn = jnp.einsum('bhqk,bkhd->bqhd', w, v)
        attn = attn.reshape(b, n, N_HEADS * HEAD_DIM)
        return attn @ Wout + bout

    def _L2_ffn_ref(x, factors, bias):
        import math
        import jax, jax.numpy as jnp
        import numpy as np
        DIM = 512
        RANK = 8
        B, T = (4, 1024)

        def _orthogonal(key, n):
            a = jax.random.normal(key, (n, n), dtype=jnp.float32)
            q, r = jnp.linalg.qr(a)
            q = q * jnp.sign(jnp.diagonal(r))[None, :]
            return q
        rank = factors.shape[0]
        mixed = jnp.einsum('btd,rde->bte', x, factors)
        mixed = mixed / math.sqrt(rank) + bias
        return mixed

    def _L3_xattn_ref(hidden_states, encoder_hidden_states, Wq, Wk, Wv, Wo, gq, gk):
        import jax, jax.numpy as jnp
        import numpy as np
        EPS = 1e-05

        def rmsnorm(x, g, eps=EPS):
            var = jnp.mean(jnp.square(x), axis=-1, keepdims=True)
            return x * jax.lax.rsqrt(var + eps) * g
        B, Sq, _ = hidden_states.shape
        Skv = encoder_hidden_states.shape[1]
        D = gq.shape[0]
        H = Wq.shape[1] // D
        scale = 1.0 / np.sqrt(D)
        q = (hidden_states @ Wq).reshape(B, Sq, H, D)
        k = (encoder_hidden_states @ Wk).reshape(B, Skv, H, D)
        v = (encoder_hidden_states @ Wv).reshape(B, Skv, H, D)
        q = rmsnorm(q, gq)
        k = rmsnorm(k, gk)
        scores = jnp.einsum('bqhd,bkhd->bhqk', q, k) * scale
        attn = jax.nn.softmax(scores, axis=-1)
        out = jnp.einsum('bhqk,bkhd->bqhd', attn, v)
        out = out.reshape(B, Sq, H * D)
        return out @ Wo

    def _L3_ffn_ref(x, router_w, router_b, expert_w, expert_b):
        import jax, jax.numpy as jnp
        import numpy as np
        NUM_EXPERTS = 16
        C = 1.0
        b, s, h = x.shape
        bs = b * s
        k = min(int(bs * C / NUM_EXPERTS), bs)
        xf = x.reshape(bs, h)
        logits = xf @ router_w + router_b
        S = jax.nn.softmax(logits, axis=-1)
        G, idx = jax.lax.top_k(S.T, k)
        tokens = xf[idx]
        out = jnp.einsum('ekh,hd->ekd', tokens, expert_w) + expert_b
        weighted = G[..., None] * out
        y = jnp.zeros((bs, h), dtype=x.dtype).at[idx.reshape(-1)].add(weighted.reshape(-1, h))
        return y.reshape(b, s, h)
    x = x + _L0_xattn_ref(_layernorm(x, axis=-1), ctx_1024, mask_BxS2_bf1, L0_xattn_Wq, L0_xattn_Wk, L0_xattn_Wv, L0_xattn_Wo)
    x = x + _L0_ffn_ref(_layernorm(x, axis=-1), L0_ffn_router_logits, L0_ffn_gating_einsum, L0_ffn_linear, L0_ffn_per_expert_scale, L0_ffn_router_scale)
    x = x + _L1_xattn_ref(_layernorm(x, axis=-1), ctx_1024, L1_xattn_Wq, L1_xattn_bq, L1_xattn_Wk, L1_xattn_bk, L1_xattn_Wv, L1_xattn_bv, L1_xattn_Wkv_dca, L1_xattn_bkv_dca, L1_xattn_qn_w, L1_xattn_qn_b, L1_xattn_kn_w, L1_xattn_kn_b, L1_xattn_kn_dca_w, L1_xattn_kn_dca_b, L1_xattn_Wo, L1_xattn_bo)
    x = x + _L1_ffn_ref(_layernorm(x, axis=-1), L1_ffn_W_up, L1_ffn_W_gate, L1_ffn_W_down)
    x = x + _L2_xattn_ref(_layernorm(x, axis=-1), ctx_1024, fside_BxSx2_0, fside_BxSx2_0, L2_xattn_Wq, L2_xattn_Wkv, L2_xattn_Wout, L2_xattn_bout)
    x = x + _L2_ffn_ref(_layernorm(x, axis=-1), L2_ffn_factors, L2_ffn_bias)
    x = x + _L3_xattn_ref(_layernorm(x, axis=-1), ctx_1024, L3_xattn_Wq, L3_xattn_Wk, L3_xattn_Wv, L3_xattn_Wo, L3_xattn_gq, L3_xattn_gk)
    x = x + _L3_ffn_ref(_layernorm(x, axis=-1), L3_ffn_router_w, L3_ffn_router_b, L3_ffn_expert_w, L3_ffn_expert_b)
    return x

_drawn_inputs = setup_inputs


def setup_inputs(seed=0):
    import zlib

    import numpy as np

    out = dict(_drawn_inputs(seed))
    spreads = {'L0_ffn_per_expert_scale': (1.0, 0.6),
     'L0_ffn_router_scale': (1.0, 0.6),
     'L1_xattn_bq': (0.0, 0.775),
     'L1_xattn_bk': (0.0, 0.317),
     'L1_xattn_bv': (0.0, 0.302),
     'L1_xattn_bkv_dca': (0.0, 0.1),
     'L1_xattn_qn_w': (1.0, 0.6),
     'L1_xattn_qn_b': (0.0, 0.8),
     'L1_xattn_kn_w': (1.0, 0.6),
     'L1_xattn_kn_b': (0.0, 0.8),
     'L1_xattn_kn_dca_w': (1.0, 0.6),
     'L1_xattn_kn_dca_b': (0.0, 0.8),
     'L1_xattn_bo': (0.0, 0.1),
     'L2_xattn_bout': (0.0, 0.1),
     'L2_ffn_bias': (0.0, 0.1),
     'L3_xattn_gq': (1.0, 0.2),
     'L3_xattn_gk': (1.0, 0.566),
     'L3_ffn_router_b': (0.0, 0.8),
     'L3_ffn_expert_b': (0.0, 0.7)}
    factors = {'L0_xattn_Wq': 7.416, 'L0_xattn_Wk': 7.436}
    for name, (base, spread) in spreads.items():
        noise = np.random.default_rng([zlib.crc32(name.encode()), seed]).standard_normal(out[name].shape)
        drawn = base * np.exp(spread * noise) if base else spread * noise
        out[name] = jnp.asarray(drawn.astype(out[name].dtype))
    for name, factor in factors.items():
        out[name] = (out[name] * factor).astype(out[name].dtype)
    return out
```

```python
import concourse.bass as bass
from concourse import mybir
from concourse.alu_op_type import AluOpType as ALU
import numpy as np

ACT = mybir.ActivationFunctionType
AX = mybir.AxisListType
F32 = mybir.dt.float32
F32R = mybir.dt.float32r
BF16 = mybir.dt.bfloat16
I32 = mybir.dt.int32
U32 = mybir.dt.uint32
U8 = mybir.dt.uint8

NB, S, D, C = 8, 256, 512, 256
T = NB * S
NT = T // 128
NBLK = 39
BASE = 16512
END = 229344


class Engine:

    def __init__(self, sem):
        self.sem, self.n, self.ops, self.seen = sem, 0, [], {}

    def wait(self, *marks):
        for m in marks:
            if m is None:
                continue
            sem, value = m
            if self.seen.get(sem.name, 0) < value:
                self.seen[sem.name] = value
                self.ops.append(lambda e, s=sem, v=value: e.wait_ge(s, v))

    def do(self, f, *waits, mark=True):
        self.wait(*waits)
        if not mark:
            self.ops.append(f)
            return None
        self.n += 1
        self.ops.append(lambda e: f(e).then_inc(self.sem, 1))
        return (self.sem, self.n)

    @property
    def last(self):
        return (self.sem, self.n) if self.n else None

    def play(self, e):
        for f in self.ops:
            f(e)


class Channel:

    def __init__(self, sem):
        self.sem, self.n = sem, 0

    def send(self, eng, f, *waits):
        eng.wait(*waits)
        self.n += 16
        eng.ops.append(lambda e: f(e).then_inc(self.sem, 16))
        return (self.sem, self.n)


class Bank:
    def __init__(self, t):
        self.t, self.free = t, []

    def __getitem__(self, k):
        return self.t[k]


class Program:
    def __init__(self, nc, ins, out, phases):
        self.nc, self.ins, self.out = nc, ins, out
        self.names = 0
        self.PE, self.A, self.V, self.G, self.SP = (Engine(self.sem(n)) for n in ("s_pe", "s_act", "s_dve", "s_pool", "s_sp"))
        self.engines = [self.PE, self.A, self.V, self.G, self.SP]
        self.channels = {}
        self.banks = [Bank(nc.alloc_psum_tensor(f"bank{i}", [128, 512], F32)) for i in range(8)]
        self.top = BASE
        self.X = self.sb("X", [128, NT, D], F32)
        self.XH = self.sb("XH", [128, 4, T], F32R)
        self.XL = self.sb("XL", [128, 4, T], F32R)
        self.xh_at, self.xl_at = BASE + 32768, BASE + 65536
        self.CTX = self.sb("CTX", [128, 2, T], F32)
        self.ident = self.sb("ident", [128, 128], F32)
        self.ones = self.sb("ones", [128, 128], F32)
        self.mhalf = self.sb("mhalf", [128, 64], F32)
        self.zero = self.sb("zero", [128, 128], F32)
        self.mv = self.sb("mv", [128, NT, 2], F32)
        self.rs = self.sb("rs", [128, NT], F32)
        self.st = self.sb("st", [128, NT, 6], F32)
        self.xn_at = self.top
        self.xn = self.sb("xn", [128, 2, D], F32)
        self.sc1 = self.sb("sc1", [128, 16], F32)
        self.arena = self.top
        self.xtok = [None] * NT
        self.phases = phases

    def sem(self, name):
        return self.nc.alloc_semaphore(name)

    def ch(self, name):
        if name not in self.channels:
            self.channels[name] = Channel(self.sem("d_" + name))
        return self.channels[name]

    def at(self, name, shape, dt, offset):
        self.names += 1
        return self.nc.alloc_sbuf_tensor_at(f"{name}_{self.names}", shape, dt, offset=offset)

    def sb(self, name, shape, dt):
        size = int(np.prod(shape[1:])) * mybir.dt.size(dt)
        t = self.at(name, shape, dt, self.top)
        self.top += -(-size // 32) * 32
        assert self.top <= END, (name, self.top - END)
        return t

    def fence(self):
        marks = [e.last for e in self.engines] + [(c.sem, c.n) for c in self.channels.values() if c.n]
        for e in self.engines:
            e.wait(*marks)
        self.top = self.arena
        for b in self.banks:
            b.free = []

    def mm(self, out, terms, *waits, mark=False, start=True, stop=True, skip=False):
        self.PE.wait(*waits)
        n = len(terms)
        for i, (l, r) in enumerate(terms):
            m = self.PE.do(
                lambda e, l=l, r=r, a=start and i == 0, z=stop and i == n - 1: e.matmul(
                    out, l, r, start=a, stop=z, skip_group_check=skip),
                mark=mark and i == n - 1)
        return m

    def transpose(self, out, in_, *waits, mark=False):
        return self.PE.do(lambda e: e.transpose(out, in_, self.ident[0:in_.shape[0], 0:in_.shape[0]]), *waits, mark=mark)

    def act(self, out, in_, func, *waits, **kw):
        return self.A.do(lambda e: e.activation(out, in_, func, **kw), *waits)

    def copy_a(self, out, in_, *waits):
        return self.act(out, in_, ACT.Copy, *waits)

    def copy_v(self, out, in_, *waits):
        return self.V.do(lambda e: e.tensor_copy(out, in_), *waits)

    def tt(self, out, a, b, op, *waits, eng=None):
        return (eng or self.V).do(lambda e: e.tensor_tensor(out, a, b, op), *waits)

    def ts(self, out, a, s1, s2, op0, op1, *waits, eng=None):
        if s2 is None:
            return (eng or self.V).do(lambda e: e.tensor_scalar(out, a, s1, None, op0), *waits)
        return (eng or self.V).do(lambda e: e.tensor_scalar(out, a, s1, s2, op0, op1), *waits)

    def stt(self, out, a, s, b, op0, op1, *waits):
        return self.V.do(lambda e: e.scalar_tensor_tensor(out, a, s, b, op0, op1), *waits)

    def red(self, out, a, op, *waits, **kw):
        return self.V.do(lambda e: e.tensor_reduce(out, a, AX.X, op, **kw), *waits)

    def rsqrt(self, out, a, *waits):
        n = a.shape[1]
        return self.tt(out, a, self.mhalf[0:a.shape[0], 0:n], ALU.pow, *waits, eng=self.G)

    def load(self, name, out, in_, *waits):
        return self.ch(name).send(self.SP, lambda e: e.dma_start(out, in_), *waits)

    def start(self):
        G, V = self.G, self.V
        a = G.do(lambda e: e.memset(self.ident[:], 0.0))
        b = G.do(lambda e: e.affine_select(out=self.ident[:], in_=self.ident[:], compare_op=ALU.not_equal, fill=1.0,
                                           base=0, pattern=[[-1, 128]], channel_multiplier=1), a)
        c = G.do(lambda e: e.memset(self.mhalf[:], -0.5))
        z = G.do(lambda e: e.memset(self.zero[:], 0.0))
        d = V.do(lambda e: e.memset(self.ones[:], 1.0))
        x = self.ins["x"].rearrange("b (t p) d -> p (b t) d", p=128)
        for h in range(4):
            m = self.load(f"x{h}", self.X[:, 4 * h:4 * h + 4, :], x[:, 4 * h:4 * h + 4, :])
            self.xtok[4 * h:4 * h + 4] = [m] * 4
        for t in range(NT):
            self.stat(t)
        m = self.load("ctx", self.CTX[:], self.ins["ctxT"])
        for e in self.engines:
            e.wait(a, b, c, d)
        self.ctxtok = m
        self.XS = self.nc.dram_tensor("rows_in", (NBLK * 128, D), F32, kind="Internal").ap()
        self.OS = self.nc.dram_tensor("rows_out", (NBLK * 128, D), F32, kind="Internal").ap()
        for q in range(4):
            self.zeroed = self.load("zero", self.XS.rearrange("(j p) d -> p j d", p=128)[:, :, 128 * q:128 * q + 128],
                                    self.zero[:].unsqueeze(1).to_broadcast([128, NBLK, 128]), z)

    def stat(self, t):
        V = self.V
        a = V.do(lambda e: e.bn_stats(self.st[:, t, :], self.X[:, t, :]), self.xtok[t])
        self.stats = V.do(lambda e: e.bn_aggr(self.mv[:, t, :], self.st[:, t, :]), a)

    def ln_all(self, keep=None, plain=None, after=None):
        a = self.ts(self.sc1[:], self.mv[:, :, 1], 1e-5, None, ALU.add, None, self.stats)
        a = self.rsqrt(self.rs[:], self.sc1[:], a)
        self.xnt, ready, turned = [None] * NT, [None] * NT, [None] * NT

        def norm(t):
            xn = self.xn[:, t % 2, :] if keep is None else keep[:, t, :]
            ready[t] = self.ts(xn, self.X[:, t, :], self.mv[:, t, 0:1], self.rs[:, t:t + 1], ALU.subtract, ALU.mult,
                               a, self.xtok[t], turned[t - 2] if t >= 2 and keep is None else None)

        def turn(t):
            xn = self.xn[:, t % 2, :] if keep is None else keep[:, t, :]
            bank = self.banks[t % 2]
            tok = slice(128 * t, 128 * t + 128)
            for k in range(4):
                p = self.transpose(bank[:, 128 * k:128 * k + 128], xn[:, 128 * k:128 * k + 128], ready[t], *bank.free, mark=k == 3)
            turned[t] = p
            src = bank[:].rearrange("p (c n) -> p c n", c=4)
            if plain is not None:
                f = (self.copy_a if t % 2 else self.copy_v)(plain[:, :, tok], src, p)
            else:
                f = self.copy_a(self.XH[:, :, tok], src, p)
                f = self.tt(self.XL[:, :, tok], src, self.XH[:, :, tok].bitcast(F32), ALU.subtract, f)
            bank.free = [f]
            self.xnt[t] = f

        norm(0)
        for t in range(NT):
            if t + 1 < NT:
                norm(t + 1)
            turn(t)
            if after is not None:
                after(t, ready[t])
        return turned[NT - 1]
    def attend_wide(self, L):
        A, V, G, PE = self.A, self.V, self.G, self.PE
        l0 = L == 0
        kh = 1 if l0 else 2
        kw = 128 * kh
        self.fence()
        self.ln_all()
        wqr = self.sb("wqr", [128, 4, 256], F32)
        wor = self.sb("wor", [128, 2, 512], F32)
        wk = self.sb("wk", [128, 2, 2, kw], F32)
        wv = self.sb("wv", [128, 2, 2, kw], F32)
        wqh, wql = (self.sb(n, [128, 2, 4, 256], F32R) for n in ("wqh", "wql"))
        woh, wol = (self.sb(n, [128, 2, 2, 512], F32R) for n in ("woh", "wol"))
        QT = self.sb("QT", [128, 2, 2, 256], F32)
        KT = self.sb("KT", [128, 2, kh, 256], F32)
        VV = self.sb("VV", [128, 2, 2, kw], F32)
        P = self.sb("P", [128, 2, 2, 256], F32)
        PT = self.sb("PT", [128, 2, 2, 2, 2, 128], F32)
        OH, OL = (self.sb(n, [128, 2, 256], F32R) for n in ("OH", "OL"))
        mx, nb, sm, rc = (self.sb(n, [128, 2, 4], F32) for n in ("mx", "nb", "sm", "rc"))
        pre = f"L{L}_xattn_"
        first = []
        if l0:
            onesb = self.sb("onesb", [1, 128], BF16)
            mu8 = self.sb("mu8", [128, T], U8)
            anym = self.sb("anym", [128, NB], F32)
            mrow = self.sb("mrow", [1, T], BF16)
            m = self.load("mask", mu8[:], self.ins["mask_BxS2_bf1"].rearrange("(a b) s -> a (b s)", a=1).to_broadcast([128, T]))
            a = self.red(anym[:], mu8[:].rearrange("p (b s) -> p b s", b=NB), ALU.max, m)
            b = self.ts(mrow[:], mu8[0:1, :], 1.0, 1e30, ALU.subtract, ALU.mult, m)
            c = V.do(lambda e: e.memset(onesb[:], 1.0))
            first = [a, b, c]
        else:
            gq = self.sb("gq", [128, 2], F32)
            m = self.load("gqk", gq[:, 0:1], self.ins["L3_xattn_gq"].rearrange("(p a) -> p a", a=1))
            m = self.load("gqk", gq[:, 1:2], self.ins["L3_xattn_gk"].rearrange("(p a) -> p a", a=1))
            gqk = self.sb("gqkp", [128, 1], F32)
            first = [self.tt(gqk[:], gq[:, 0:1], gq[:, 1:2], ALU.mult, m)]
            K1 = self.sb("K1", [128, 4, 128], F32)
            sq = self.sb("sq", [128, 512], F32)
            q2 = self.sb("q2", [128, 2, 256], F32)
            kst = self.sb("kst", [128, 3, 4], F32)
            qst = self.sb("qst", [128, 2, 4], F32)
        SC = 128.0 ** -0.5
        loaded, split = {}, {}
        done = {}

        def fetch(g):
            s, w = split.get(g - 1), done.get(("kv", g - 2))
            a = self.load("wq", wqr[:], self.ins[pre + "Wq"][g], s and s[0])
            b = self.load(f"wk{g % 2}", wk[:, g % 2, :, :], self.ins[pre + "Wk"][g], w)
            b = self.load(f"wk{g % 2}", wv[:, g % 2, :, :], self.ins[pre + "Wv"][g], w)
            c = self.load("wo", wor[:], self.ins[pre + "Wo"][g], s and s[1])
            loaded[g] = (a, b, c)

        def part(g):
            a, _, c = loaded[g]
            j = g % 2
            h = self.copy_a(wqh[:, j, :, :], wqr[:], a, done.get(("q", g - 2)))
            q = self.tt(wql[:, j, :, :], wqr[:], wqh[:, j, :, :].bitcast(F32), ALU.subtract, h)
            h = self.copy_a(woh[:, j, :, :], wor[:], c, done.get(("y", g - 2)))
            o = self.tt(wol[:, j, :, :], wor[:], woh[:, j, :, :].bitcast(F32), ALU.subtract, h)
            split[g] = (q, o)

        units = [(g, b) for g in range(8) for b in range(NB)]
        turn = [0]

        def bank_a():
            turn[0] += 1
            return self.banks[turn[0] % 2]

        sb_, tb, ob, yb = self.banks[2:4], self.banks[4:6], self.banks[6], self.banks[7]
        R = {}

        def proj(u):
            g, b = units[u]
            j, w = u % 2, g % 2
            if b == 0 and g + 1 < 8:
                fetch(g + 1)
            if b == 5 and g + 1 < 8:
                part(g + 1)
            if b == 0:
                R["xw"] = split[g][0]
            tok = slice(256 * b, 256 * b + 256)
            k = bank_a()
            if l0:
                m = self.mm(k[:, 0:256], [(wk[:, w, c, :], self.CTX[:, c, tok]) for c in range(2)],
                            self.ctxtok, loaded[g][1], *k.free)
                for i in range(2):
                    tk = slice(256 * b + 128 * i, 256 * b + 128 * i + 128)
                    m = self.mm(k[:, 256 + 128 * i:384 + 128 * i],
                                [(self.CTX[:, c, tk], wv[:, w, c, :]) for c in range(2)], mark=i == 1)
                f = self.copy_v(KT[:, j, 0, :], k[:, 0:256], m, R.get(("S", u - 2)))
                f = self.copy_v(VV[:, j, :, :], k[:, 256:512].rearrange("p (t n) -> p t n", t=2), R.get(("O", u - 2)))
                k.free = [f]
                R["k", u] = f
            else:
                for i in range(2):
                    tk = slice(256 * b + 128 * i, 256 * b + 128 * i + 128)
                    m = self.mm(k[:, 256 * i:256 * i + 256], [(self.CTX[:, c, tk], wk[:, w, c, :]) for c in range(2)],
                                self.ctxtok, loaded[g][1], *k.free, mark=i == 1)
                f = self.act(sq[:], k[:], ACT.Square, m, R.get("sq"))
                s = self.red(kst[:, 0, :], sq[:].rearrange("p (t n) -> p t n", t=4), ALU.add, f, R.get("kr"))
                R["sq"] = s
                s = self.ts(kst[:, 1, :], kst[:, 0, :], 1.0 / 128, 1e-5, ALU.mult, ALU.add, s)
                s = self.rsqrt(kst[:, 2, :], kst[:, 1, :], s)
                f = self.tt(K1[:], k[:].rearrange("p (t n) -> p t n", t=4),
                            kst[:, 2, :].unsqueeze(2).to_broadcast([128, 4, 128]), ALU.mult, s, R.get("kt"))
                R["kr"] = f
                k.free = [f]
                R["k1", u] = f
            z = bank_a()
            for h in range(2):
                cs = slice(128 * h, 128 * h + 128)
                terms = []
                for c in range(4):
                    xh, xl = self.XH[:, c, tok], self.XL[:, c, tok]
                    terms += [(wqh[:, w, c, cs], xh), (wqh[:, w, c, cs], xl), (wql[:, w, c, cs], xh)]
                m = self.mm(z[:, 256 * h:256 * h + 256], terms, self.xnt[2 * b], self.xnt[2 * b + 1], split[g][0],
                            *z.free, mark=h == 1)
            done[("q", g)] = mq = m
            zz = z[:].rearrange("p (h n) -> p h n", h=2)
            f = self.copy_a(QT[:, j, :, :], zz, mq, R.get(("S", u - 2)))
            if not l0:
                f = self.act(q2[:], zz, ACT.Square, m, R.get(("qs", u - 1)))
            z.free = [f]
            R["q", u] = f
            if not l0:
                v = bank_a()
                for i in range(2):
                    tk = slice(256 * b + 128 * i, 256 * b + 128 * i + 128)
                    m = self.mm(v[:, 256 * i:256 * i + 256], [(self.CTX[:, c, tk], wv[:, w, c, :]) for c in range(2)],
                                *v.free, mark=i == 1)
                f = self.copy_v(VV[:, j, :, :], v[:].rearrange("p (t n) -> p t n", t=2), m, R.get(("O", u - 2)))
                v.free = [f]
                R["v", u] = f
            done[("kv", g)] = self.PE.last

        def late(u):
            j = u % 2
            k = bank_a()
            for i in range(2):
                for h in range(2):
                    m = self.transpose(k[:, 256 * h + 128 * i:256 * h + 128 * i + 128], K1[:, 2 * i + h, :],
                                       R["k1", u], *k.free, mark=i + h == 2)
            R["kt"] = m
            f = self.act(KT[:, j, :, :], k[:].rearrange("p (h n) -> p h n", h=2), ACT.Copy, m, R.get(("S", u - 2)),
                         *first, scale=gqk[:, 0:1])
            k.free = [f]
            R["k", u] = f
            z = bank_a()
            for qt in range(2):
                for h in range(2):
                    m = self.mm(z[:, 2 * qt + h:2 * qt + h + 1],
                                [(q2[:, h, 128 * qt:128 * qt + 128], self.ones[:, 0:1])], R["q", u], *z.free,
                                mark=qt + h == 2)
            R["qs", u] = m
            f = self.ts(qst[:, 0, :], z[:, 0:4], 128e-5, None, ALU.add, None, m, R.get("qr"))
            z.free = [f]
            f = self.rsqrt(qst[:, 1, :], qst[:, 0, :], f, R.get(("E", u - 1)))
            R["qr"] = f

        def scores(u):
            g, b = units[u]
            j = u % 2
            for qt in range(2):
                z = sb_[qt]
                if l0:
                    mb = mrow[0:1, 256 * b:256 * b + 256].unsqueeze(1).to_broadcast([1, 2, 256])
                    self.mm(z[:].rearrange("p (h n) -> p h n", h=2), [(onesb[:], mb)], *first, *z.free, stop=False, skip=True)
                for h in range(2):
                    m = self.mm(z[:, 256 * h:256 * h + 256],
                                [(QT[:, j, h, 128 * qt:128 * qt + 128], KT[:, j, 0 if l0 else h, :])],
                                R["q", u], R["k", u], *z.free, start=not l0, skip=l0, mark=h == 1)
                c = slice(2 * qt, 2 * qt + 2)
                s = self.red(mx[:, j, c], z[:].rearrange("p (h n) -> p h n", h=2), ALU.max, m, R.get(("N", u - 2)), negate=True)
                if l0:
                    s = self.ts(nb[:, j, c], mx[:, j, c], SC, None, ALU.mult, None, s, R.get(("E", u - 2)))
                else:
                    s = self.tt(nb[:, j, c], mx[:, j, c], qst[:, 1, c], ALU.mult, s, R["qr"], R.get(("E", u - 2)))
                for h in range(2):
                    i = 2 * qt + h
                    f = self.act(P[:, qt, h, :], z[:, 256 * h:256 * h + 256], ACT.Exp, s, R.get(("T", u - 1)),
                                 R.get(("N", u - 2)), bias=nb[:, j, i:i + 1], scale=SC if l0 else qst[:, 1, i:i + 1],
                                 accum_out=sm[:, j, i:i + 1])
                z.free = [f]
            R["S", u] = m
            R["E", u] = f

        def norm(u):
            g, b = units[u]
            j = u % 2
            r = V.do(lambda e: e.reciprocal(rc[:, j, :], sm[:, j, :]), R["E", u])
            if l0:
                r = self.ts(rc[:, j, :], rc[:, j, :], anym[:, b:b + 1], None, ALU.mult, None, r)
            for qt in range(2):
                for h in range(2):
                    i = 2 * qt + h
                    r2 = self.ts(P[:, qt, h, :], P[:, qt, h, :], rc[:, j, i:i + 1], None, ALU.mult, None, r)
            R["N", u] = r2

        def turn_p(u):
            j = u % 2
            fs = []
            for qt in range(2):
                z = tb[qt]
                for kt in range(2):
                    for h in range(2):
                        i = 2 * kt + h
                        m = self.transpose(z[:, 128 * i:128 * i + 128], P[:, qt, h, 128 * kt:128 * kt + 128],
                                           R["N", u], *z.free, mark=i == 3)
                out = PT[:, j, qt, :, :, :].rearrange("p k h n -> p (k h n)")
                f = (self.copy_a if qt == 0 else self.copy_v)(out, z[:], m, R.get(("O", u - 2)))
                z.free = [f]
                fs.append(f)
            R["T", u] = m
            R["pt", u] = fs

        def pv(u):
            j = u % 2
            z = ob
            for h in range(2):
                vs = slice(0, 128) if l0 else slice(128 * h, 128 * h + 128)
                m = self.mm(z[:, 256 * h:256 * h + 256].rearrange("p (q n) -> p q n", q=2),
                            [(VV[:, j, kt, vs], PT[:, j, :, kt, h, :]) for kt in range(2)],
                            *R["pt", u], R["k" if l0 else "v", u], *z.free, mark=h == 1)
            R["O", u] = m
            zz = z[:].rearrange("p (h n) -> p h n", h=2)
            f = self.copy_a(OH[:], zz, m, R.get(("Y", u - 1)))
            f = self.tt(OL[:], zz, OH[:].bitcast(F32), ALU.subtract, f)
            z.free = [f]
            R["o", u] = f

        def outp(u):
            g, b = units[u]
            w = g % 2
            for i in range(2):
                z = yb
                ts = slice(128 * i, 128 * i + 128)
                terms = []
                for h in range(2):
                    terms += [(OH[:, h, ts], woh[:, w, h, :]), (OH[:, h, ts], wol[:, w, h, :]), (OL[:, h, ts], woh[:, w, h, :])]
                m = self.mm(z[:], terms, R["o", u], split[g][1], *z.free, mark=True)
                x = self.X[:, 2 * b + i, :]
                f = self.tt(x, x, z[:], ALU.add, m, self.xtok[2 * b + i])
                z.free = [f]
                self.xtok[2 * b + i] = f
            R["Y", u] = m
            done[("y", g)] = m
            if g == 7:
                self.stat(2 * b)
                self.stat(2 * b + 1)

        n = len(units)
        fetch(0)
        part(0)
        proj(0)
        if not l0:
            late(0)
        scores(0)
        norm(0)
        for u in range(n):
            if u + 1 < n:
                proj(u + 1)
            turn_p(u)
            if u + 1 < n:
                if not l0:
                    late(u + 1)
                scores(u + 1)
            if u >= 1:
                outp(u - 1)
            pv(u)
            if u + 1 < n:
                norm(u + 1)
        outp(n - 1)
    def bcast(self, name, t, src):
        n = int(np.prod(src.shape))
        return self.load(name, t, src.rearrange("(a n) -> a n", a=1).to_broadcast([128, n]))

    def split_w(self, raw, hi, lo, *waits):
        f = self.copy_a(hi, raw, *waits)
        return self.tt(lo, raw, hi.bitcast(F32), ALU.subtract, f)

    def ternary_ffn(self):
        V, A, G = self.V, self.A, self.G
        self.fence()
        raw = self.sb("raw", [128, 2, 4, 512], F32)
        TT = [self.sb(n, [128, 2, 4, 512], F32R) for n in ("Tu", "Tg", "Td")]
        neg = self.sb("neg", [128, 512], F32)
        HH, HL = (self.sb(n, [128, 2, 4, 256], F32R) for n in ("HH", "HL"))
        sl = self.sb("sl", [128, 512], F32)
        hf = self.sb("hf", [128, 2, 512], F32)
        s12 = self.sb("s12", [128, 12], F32)
        s3 = self.sb("s3", [128, 6, 3], F32)
        names = ["L1_ffn_W_up", "L1_ffn_W_gate", "L1_ffn_W_down"]
        free = [None, None]
        for i in range(12):
            j = i % 2
            m = self.load(f"raw{j}", raw[:, j, :, :], self.ins[names[i // 4]][i % 4], free[j])
            r = raw[:, j, :, :].rearrange("p c n -> p (c n)")
            free[j] = a = self.act(r, r, ACT.Abs, m, accum_out=s12[:, i:i + 1])
        s = self.red(s3[:, 0, :], s12[:].rearrange("p (w g) -> p w g", w=3), ALU.add, a)
        z = self.banks[2]
        m = self.mm(z[:, 0:3], [(self.ones[:], s3[:, 0, :])], s, mark=True)
        scale, half, nhalf, sgd = s3[:, 1, :], s3[:, 2, :], s3[:, 3, :], s3[:, 4, 0:1]
        s = self.ts(scale, z[:, 0:3], 2.0 ** -20, 1e-8, ALU.mult, ALU.add, m)
        z.free = [s]
        a = self.ts(half, scale, 0.5, None, ALU.mult, None, s)
        b = self.ts(nhalf, scale, -0.5, None, ALU.mult, None, s)
        scaled = self.tt(sgd, scale[:, 1:2], scale[:, 2:3], ALU.mult, s)
        self.ln_all()
        tern, done, R = {}, {}, {"raw": 0, "neg": None}

        def make(g):
            marks = []
            for w in range(3):
                j = R["raw"] % 2
                R["raw"] += 1
                m = self.load(f"raw{j}", raw[:, j, :, :], self.ins[names[w]][g], free[j])
                for c in range(4):
                    r = raw[:, j, c, :]
                    a = self.ts(neg[:], r, nhalf[:, w:w + 1], None, ALU.is_lt, None, m, R["neg"], scaled)
                    b = self.stt(TT[w][:, g % 2, c, :], r, half[:, w:w + 1], neg[:], ALU.is_gt, ALU.subtract, a,
                                 done.get((w, g - 2)))
                    R["neg"] = b
                free[j] = b
                marks.append(b)
            tern[g] = marks

        units = [(g, b) for g in range(4) for b in range(NB)]
        ub, gb, yb = self.banks[2:4], self.banks[4:6], self.banks[6:8]

        def up(u):
            g, b = units[u]
            w, j = g % 2, u % 2
            tok = slice(256 * b, 256 * b + 256)
            for cp in range(2):
                for W, z in ((0, ub[cp]), (1, gb[cp])):
                    for i in range(2):
                        hid = slice(256 * cp + 128 * i, 256 * cp + 128 * i + 128)
                        terms = []
                        for c in range(4):
                            t = TT[W][:, w, c, hid]
                            terms += [(t, self.XH[:, c, tok]), (t, self.XL[:, c, tok])]
                        m = self.mm(z[:, 256 * i:256 * i + 256], terms, tern[g][W], self.xnt[2 * b], self.xnt[2 * b + 1],
                                    *z.free, mark=i == 1)
                    done[(W, g)] = m
                    if W == 0:
                        f = self.act(sl[:], z[:], ACT.Silu, m, R.get("sl"), scale=scale[:, 0:1])
                        z.free = [f]
                p = cp
                f = self.stt(hf[:, p, :], gb[cp][:], sgd, sl[:], ALU.mult, ALU.mult, m, f, R.get(("hf", p)))
                gb[cp].free = [f]
                R["sl"] = f
                hh = HH[:, j, 2 * cp:2 * cp + 2, :].rearrange("p c n -> p (c n)")
                hl = HL[:, j, 2 * cp:2 * cp + 2, :].rearrange("p c n -> p (c n)")
                f = self.copy_a(hh, hf[:, p, :], f, R.get(("down", u - 2)))
                f = self.tt(hl, hf[:, p, :], hh.bitcast(F32), ALU.subtract, f, R.get(("down", u - 2)), eng=G)
                R["hf", p] = f
            R["h", u] = f

        def down(u):
            g, b = units[u]
            w, j = g % 2, u % 2
            for i in range(2):
                z = yb[i]
                ts = slice(128 * i, 128 * i + 128)
                terms = []
                for c in range(4):
                    t = TT[2][:, w, c, :]
                    terms += [(HH[:, j, c, ts], t), (HL[:, j, c, ts], t)]
                m = self.mm(z[:], terms, R["h", u], tern[g][2], *z.free, mark=True)
                x = self.X[:, 2 * b + i, :]
                f = self.tt(x, x, z[:], ALU.add, m, self.xtok[2 * b + i])
                z.free = [f]
                self.xtok[2 * b + i] = f
                if g == 3:
                    self.stat(2 * b + i)
            R["down", u] = m
            done[(2, g)] = m

        make(0)
        up(0)
        for u in range(len(units)):
            if u % 8 == 2 and u // 8 < 3:
                make(u // 8 + 1)
            if u + 1 < len(units):
                up(u + 1)
            down(u)

    def mix(self):
        V = self.V
        self.fence()
        raw = self.sb("raw", [128, 2, 4, 512], F32)
        acc = self.sb("acc", [128, 4, 512], F32)
        fh, fl = (self.sb(n, [128, 4, 512], F32R) for n in ("fh", "fl"))
        bias = self.sb("bias", [128, 512], F32)
        tmp = self.sb("tmp", [128, 2, 512], F32)
        mb = self.bcast("bias", bias[:], self.ins["L2_ffn_bias"])
        free = [None, None]
        f = self.load("raw2", acc[:], self.ins["L2_ffn_factors"][0])
        for r in range(1, 8):
            j = r % 2
            m = self.load(f"raw{j}", raw[:, j, :, :], self.ins["L2_ffn_factors"][r], free[j])
            f = free[j] = self.tt(acc[:], acc[:], raw[:, j, :, :], ALU.add, m, f, eng=self.V)
        w = self.split_w(acc[:], fh[:], fl[:], f)
        self.ln_all()
        done = {}
        for t in range(NT):
            z = self.banks[2 + t % 4]
            tok = slice(128 * t, 128 * t + 128)
            terms = []
            for c in range(4):
                xh, xl = self.XH[:, c, tok], self.XL[:, c, tok]
                terms += [(xh, fh[:, c, :]), (xh, fl[:, c, :]), (xl, fh[:, c, :])]
            m = self.mm(z[:], terms, w, self.xnt[t], *z.free, mark=True)
            a = self.stt(tmp[:, t % 2, :], z[:], 8.0 ** -0.5, bias[:], ALU.mult, ALU.add, m, mb, done.get(t - 2))
            z.free = [a]
            x = self.X[:, t, :]
            done[t] = self.xtok[t] = self.tt(x, x, tmp[:, t % 2, :], ALU.add, a, self.xtok[t], eng=self.G)
            if t >= 2:
                self.stat(t - 2)
        self.stat(NT - 2)
        self.stat(NT - 1)

    def choice(self):
        V, A = self.V, self.A
        self.fence()
        raw = self.sb("raw", [128, 4, 512], F32)
        wh, wl = (self.sb(n, [128, 4, 512], F32R) for n in ("wh", "wl"))
        rr = self.sb("rr", [128, 4, 16], F32)
        rh, rl = (self.sb(n, [128, 4, 16], F32R) for n in ("rh", "rl"))
        rb = self.sb("rb", [128, 16], F32)
        eb = self.sb("eb", [128, 512], F32)
        Y = self.sb("Y", [128, NT, 512], F32)
        LG = self.sb("LG", [128, NT, 16], F32)
        sm = self.sb("sm", [128, 3, NT], F32)
        ST = self.sb("ST", [16, T], F32)
        WK = self.sb("WK", [16, T], F32)
        m8 = self.sb("m8", [16, 2, 8], F32)
        cc = self.sb("cc", [128, NT], F32)
        m1 = self.load("raw0", raw[:], self.ins["L3_ffn_expert_w"])
        m2 = self.load("raw1", rr[:], self.ins["L3_ffn_router_w"])
        m3 = self.bcast("rb", rb[:], self.ins["L3_ffn_router_b"])
        m4 = self.bcast("eb", eb[:], self.ins["L3_ffn_expert_b"])
        r = self.split_w(rr[:], rh[:], rl[:], m2)
        w = self.split_w(raw[:], wh[:], wl[:], m1)
        self.ln_all()
        for t in range(NT):
            z = self.banks[2 + t % 2]
            tok = slice(128 * t, 128 * t + 128)
            terms = []
            for c in range(4):
                xh, xl = self.XH[:, c, tok], self.XL[:, c, tok]
                terms += [(xh, rh[:, c, :]), (xh, rl[:, c, :]), (xl, rh[:, c, :])]
            m = self.mm(z[:, 0:16], terms, r, self.xnt[t], *z.free, mark=True)
            f = self.tt(LG[:, t, :], z[:, 0:16], rb[:], ALU.add, m, m3)
            z.free = [f]
        s = self.red(sm[:, 0, :], LG[:], ALU.max, f)
        s = self.tt(LG[:], LG[:], sm[:, 0, :].unsqueeze(2).to_broadcast([128, NT, 16]), ALU.subtract, s)
        s = self.act(LG[:], LG[:], ACT.Exp, s)
        a = self.red(sm[:, 1, :], LG[:], ALU.add, s)
        a = V.do(lambda e: e.reciprocal(sm[:, 2, :], sm[:, 1, :]), a)
        s = self.tt(LG[:], LG[:], sm[:, 2, :].unsqueeze(2).to_broadcast([128, NT, 16]), ALU.mult, a)
        for k in range(4):
            z = self.banks[2 + k % 2]
            for i in range(4):
                m = self.transpose(z[0:16, 128 * i:128 * i + 128], LG[:, 4 * k + i, :], s, *z.free, mark=i == 3)
            f = self.copy_a(ST[:, 512 * k:512 * k + 512], z[0:16, :], m)
            z.free = [f]
        for t in range(NT):
            z = self.banks[4 + t % 2]
            tok = slice(128 * t, 128 * t + 128)
            terms = []
            for c in range(4):
                xh, xl = self.XH[:, c, tok], self.XL[:, c, tok]
                terms += [(xh, wh[:, c, :]), (xh, wl[:, c, :]), (xl, wh[:, c, :])]
            m = self.mm(z[:], terms, w, *z.free, mark=True)
            y = self.copy_a(Y[:, t, :], z[:], m)
            z.free = [y]
            y = self.tt(Y[:, t, :], Y[:, t, :], eb[:], ALU.add, y, m4, eng=self.G)
        cur = ST
        o = None
        for i in range(16):
            a = V.do(lambda e, i=i, cur=cur: e.max(m8[:, i % 2, :], cur[:]), f)
            f = V.do(lambda e, i=i, cur=cur: e.match_replace(WK[:], m8[:, i % 2, :], cur[:], -1.0), a)
            cur = WK
        f = self.stt(ST[:], WK[:], 0.0, ST[:], ALU.is_lt, ALU.mult, f)
        z = self.banks[2]
        for t in range(NT):
            m = self.mm(z[:, t:t + 1], [(ST[:, 128 * t:128 * t + 128], self.ones[0:16, 0:1])], f, *z.free, mark=t == NT - 1)
        f = self.copy_v(cc[:], z[:, 0:NT], m)
        z.free = [f]
        for t in range(NT):
            x = self.X[:, t, :]
            self.xtok[t] = self.stt(x, Y[:, t, :], cc[:, t:t + 1], x, ALU.mult, ALU.add, f, y, self.xtok[t])

    def attend_narrow(self, L):
        A, V, G, PE = self.A, self.V, self.G, self.PE
        l1 = L == 1
        H, HD = (16, 32) if l1 else (32, 16)
        SC = float(HD) ** -0.5
        NP_ = H // 2
        self.fence()
        XF = self.at("XF", [128, 4, T], F32, self.xh_at)
        xl = [self.xl_at]

        def side(name, shape, dt):
            t = self.at(name, shape, dt, xl[0])
            xl[0] += -(-int(np.prod(shape[1:])) * mybir.dt.size(dt) // 32) * 32
            assert xl[0] <= self.xl_at + 32768
            return t

        pre = f"L{L}_xattn_"
        wq = self.sb("nwq", [128, 4, 512], F32)
        wkv = self.sb("nwkv", [128, 2, 1024], F32)
        wo = self.sb("nwo", [128, 4, 512], F32)
        kT = [self.sb("kT0", [128, 16, 256], F32R), None]
        over = xl[0]
        kT[1] = side("kT1", [128, 16, 256], F32R)
        bo = side("nbo", [128, 512], F32)
        qT = self.sb("nqT", [128, 2, 16, 128], F32R)
        stk = self.sb("stk", [128, 16, 128], F32R)
        VV = self.sb("nV", [128, 2, 2, 32 * H], F32)
        PT = self.sb("nPT", [128, 2, 4, 128], F32)
        OT = self.sb("nOT", [128, 4, 128], F32)
        cbk = [self.sb("ncb0", [128, 512], F32), side("ncb1", [128, 512], F32)]
        st4 = self.sb("nst", [128, 4, 16], F32)
        mx, nb, sm, rc = (self.sb(n, [128, 5, 4], F32) for n in ("nmx", "nnb", "nsm", "nrc"))
        depth, np_ = 3, 4
        more = [(self.sb if l1 else side)(f"nP{i}", [128, 2, 256], F32) for i in range(2, np_)]
        mq = self.load("raw0", wq[:], self.ins[pre + "Wq"])
        mk = self.load("raw1", wkv[:], self.ins[pre + "Wkv"])
        mo = self.load("wo", wo[:], self.ins[pre + ("Wo" if l1 else "Wout")])
        mbo = self.bcast("bias", bo[:], self.ins[pre + ("bo" if l1 else "bout")])
        R = {}
        if l1:
            bkv = self.sb("nbkv", [128, 1024], F32)
            bq = side("nbq", [128, 512], F32)
            kdT = side("kdT", [128, 16, 128], F32R)
            Vd = side("Vd", [128, 512], F32)
            cd = self.at("ncd", [128, 2, 128], F32, over + 12288)
            wd = self.at("nwd", [128, 2, 1024], F32, over)
            bd = self.at("nbd", [128, 1024], F32, over + 8192)
            vec = {n: self.sb("v" + n, [128, 32], F32) for n in ("qn_w", "qn_b", "kn_w", "kn_b", "kn_dca_w", "kn_dca_b")}
            md = self.load("wd", wd[:], self.ins[pre + "Wkv_dca"])
            mc = self.load("cd", cd[:], self.ins["ctx_dcaT"])
            mb = self.bcast("b1", bd[:], self.ins[pre + "bkv_dca"])
            mb = self.bcast("b1", bkv[:, 0:512], self.ins[pre + "bk"])
            mb = self.bcast("b1", bkv[:, 512:1024], self.ins[pre + "bv"])
            mb = self.bcast("b1", bq[:], self.ins[pre + "bq"])
            for n, t in vec.items():
                mb = self.bcast("b1", t[:], self.ins[pre + n])
        else:
            pos = side("pos", [128, NT, 2], F32)
            ang = self.at("ang", [128, NT, 2, 4], F32, over)
            kk = self.at("kk", [128, NT * 8], F32, over + 512)
            rr = self.at("rr", [128, NT * 8], F32, over + 1024)
            cs = [side(n, [128, NT, 8], F32) for n in ("cosT", "sinT")]
            m1b = side("m1b", [128, 512], F32)
            m2b = side("m2b", [128, 512], F32)
            m = self.load("b1", pos[:], self.ins["fside_BxSx2_0"].rearrange("b (t p) c -> p (b t) c", p=128))
            freqs = np.float32(10000.0) ** (-np.arange(4, dtype=np.float32) / np.float32(4))
            for j in range(4):
                a = self.ts(ang[:, :, :, j], pos[:], float(freqs[j]), None, ALU.mult, None, m)
            ang = ang[:].rearrange("p t c j -> p (t c j)")
            c1 = np.float32(6.28125)
            c2 = np.float32(2 * np.pi - 6.28125)
            c3 = np.float32(2 * np.pi - 6.28125 - float(c2))
            for w, (quarter, shift) in enumerate(((0.25, np.pi / 2), (0.0, 0.0))):
                a = self.ts(kk[:], ang, 1 / (2 * np.pi), quarter, ALU.mult, ALU.add, a)
                a = self.ts(kk[:], kk[:], 12582912.0, 12582912.0, ALU.add, ALU.subtract, a)
                a = self.stt(rr[:], kk[:], -float(c1), ang, ALU.mult, ALU.add, a)
                a = self.stt(rr[:], kk[:], -float(c2), rr[:], ALU.mult, ALU.add, a)
                a = self.stt(rr[:], kk[:], -float(c3), rr[:], ALU.mult, ALU.add, a)
                a = self.ts(rr[:], rr[:], float(shift), 3.1415925, ALU.add, ALU.min, a)
                a = self.ts(rr[:], rr[:], -3.1415925, None, ALU.max, None, a)
                a = self.act(cs[w][:].rearrange("p t c -> p (t c)"), rr[:], ACT.Sin, a)
            mb = a
        cen = None
        if l1:
            def center(v, n, *waits):
                m = avg[:, 0:n]
                a = self.red(m, v, ALU.add, *waits)
                a = self.ts(m, m, 1.0 / 32, None, ALU.mult, None, a)
                return self.tt(v, v, m.unsqueeze(2).to_broadcast([128, n, 32]), ALU.subtract, a)

            avg = st4[:].rearrange("p a h -> p (a h)")
            cols = lambda v: v.rearrange("p (h d) -> p h d", d=32)
            cen = center(wq[:].rearrange("p c (h d) -> p (c h) d", d=32), 64, mq)
            cen = center(wkv[:].rearrange("p c (h e d) -> p (c h) e d", e=2, d=32)[:, :, 0, :], 32, mk, cen)
            for c in range(2):
                cen = center(cols(wd[:, c, 0:512]), 16, md, cen)
            cen = center(cols(bd[:, 0:512]), 16, mb, cen)
            cen = center(cols(bq[:]), 16, cen)
            cen = center(bkv[:].rearrange("p (h e d) -> p h e d", e=2, d=32)[:, :, 0, :], 16, cen)
        xn_free = self.ln_all(plain=XF)
        Pb = [self.at(f"nP{i}", [128, 2, 256], F32, self.xn_at + 2048 * i) for i in range(2)] + more

        pbank, tbank = self.banks[0], self.banks[1]

        def old(*key):
            return R[key] if key[1] >= 0 else None

        wide = lambda v: v[:].rearrange("p (h d) -> p h d", d=HD)

        def square(src, z, f, k):
            f = self.act(z[:], src, ACT.Square, f)
            yield
            f = self.red(st4[:, k, :], z[:].rearrange("p (h d) -> p h d", h=16), ALU.add, f)
            z.free = [f]
            f = self.ts(st4[:, k, :], st4[:, k, :], 1.0 / 32, 1e-6, ALU.mult, ALU.add, f)
            f = self.rsqrt(st4[:, k + 1, :], st4[:, k, :], f)
            yield
            return f

        def scale(c3, w, b, f, k):
            g = 16 // c3.shape[1] if len(c3.shape) == 4 else 0
            rs = st4[:, k + 1, :]
            if g:
                rs = rs.rearrange("p (c h) -> p c h", h=g).unsqueeze(3).to_broadcast(list(c3.shape))
                row = lambda v: v[:].unsqueeze(1).unsqueeze(1).to_broadcast(list(c3.shape))
            else:
                rs = rs.unsqueeze(2).to_broadcast(list(c3.shape))
                row = lambda v: v[:].unsqueeze(1).to_broadcast(list(c3.shape))
            f = self.tt(c3, c3, rs, ALU.mult, f)
            f = self.tt(c3, c3, row(w), ALU.mult, f, mb, eng=G)
            return self.tt(c3, c3, row(b), ALU.add, f, eng=G)

        def rope(t, z, m, oo, *free):
            zz = z[:].rearrange("p (h c d) -> p h c d", h=32, d=2)
            m1, m2 = (x[:].rearrange("p (h c d) -> p h c d", h=32, d=2) for x in (m1b, m2b))
            f = None
            for d in range(2):
                tab = lambda w: cs[w][:, t, :].unsqueeze(1).to_broadcast([128, 32, 8])
                self.tt(m1[:, :, :, d], zz[:, :, :, d], tab(0), ALU.mult, m, mb, R.get("rope"))
                f = self.tt(m2[:, :, :, d], zz[:, :, :, d], tab(1), ALU.mult)
            z.free = [f]
            yield
            g = self.tt(oo(0), halves(m1, 0), halves(m2, 1), ALU.subtract, f, *free, eng=G)
            g = self.tt(oo(1), halves(m2, 0), halves(m1, 1), ALU.add, f, eng=G)
            R["rope"] = g
            yield
            return g

        def halves(m, d):
            return m[:, :, :, d].rearrange("p (c h) e -> p c h e", c=4)

        def project(w, x, *waits):
            n = len(x)
            for c in range(n):
                m = self.mm(pbank[:], [(x[c], w(c))], *waits, *pbank.free, mark=c == n - 1, start=c == 0, stop=c == n - 1)
                if c % 2:
                    yield
            return m

        def norm_q(t):
            tok = slice(128 * t, 128 * t + 128)
            z = pbank
            m = yield from project(lambda c: wq[:, c, :], [XF[:, c, tok] for c in range(4)], mq, cen, self.xnt[t])
            q = XF[:, :, tok]
            if l1:
                f = self.tt(q, z[:].rearrange("p (c n) -> p c n", c=4), bq[:].rearrange("p (c n) -> p c n", c=4), ALU.add, m, mb)
                yield
                f = yield from square(q, z, f, 0)
                yield
                f = scale(q.rearrange("p c (h d) -> p c h d", d=32), vec["qn_w"], vec["qn_b"], f, 0)
            else:
                qq = q.rearrange("p c (h e d) -> p c h e d", e=8, d=2)
                f = yield from rope(t, z, m, lambda d: qq[:, :, :, :, d])
            R["qn", t] = f
            yield

        def norm_k(t):
            tok = slice(128 * t, 128 * t + 128)
            z, cb = pbank, cbk[t % 2]
            free = R.get(("kd", t - 2), [])
            if l1:
                w = lambda c: wkv[:, c, :].rearrange("p (h e d) -> p h e d", e=2, d=32)[:, :, 0, :]
            else:
                w = lambda c: wkv[:, c, 0:512]
            m = yield from project(w, [self.CTX[:, c, tok] for c in range(2)], mk, cen, self.ctxtok)
            if l1:
                f = self.tt(wide(cb), wide(z.t), bkv[:].rearrange("p (h e d) -> p h e d", e=2, d=32)[:, :, 0, :], ALU.add, m, mb, *free)
                yield
                f = yield from square(cb[:], z, f, 2)
                yield
                f = scale(wide(cb), vec["kn_w"], vec["kn_b"], f, 2)
            else:
                kk_ = cb[:].rearrange("p (c h e d) -> p c h e d", c=4, e=8, d=2)
                f = yield from rope(t, z, m, lambda d: kk_[:, :, :, :, d], *free)
            R["kn", t] = f
            yield

        def values(t):
            b, i = t // 2, t % 2
            j = b % 2
            tok = slice(128 * t, 128 * t + 128)
            z = pbank
            if l1:
                w = lambda c: wkv[:, c, :].rearrange("p (h e d) -> p h e d", e=2, d=32)[:, :, 1, :]
            else:
                w = lambda c: wkv[:, c, 512:1024]
            m = yield from project(w, [self.CTX[:, c, tok] for c in range(2)], mk, self.ctxtok)
            if l1:
                f = self.tt(wide(VV[:, j, i, :]), wide(z.t), bkv[:].rearrange("p (h e d) -> p h e d", e=2, d=32)[:, :, 1, :],
                            ALU.add, m, mb, old("O", b - 2))
                if i == 1:
                    R["v", b, 1] = self.load(f"vd{j}", VV[112:128, j, 1, :], Vd[16 * b:16 * b + 16, :], f, R["vd"])
                else:
                    R["v", b, 0] = f
            else:
                for e in range(2):
                    vv = VV[:, j, i, :].rearrange("p (h e d) -> p h e d", e=2, d=32)[:, :, e, 16 * e:16 * e + 16]
                    f = self.copy_a(vv, z[:].rearrange("p (h e d) -> p h e d", e=2, d=16)[:, :, e, :], m, old("O", b - 2), cleared)
                R["v", b, i] = f
            z.free = [f]
            yield

        def stack(f, src, queries, dst, n, *free):
            if len(src.shape) == 4:
                v = stk[:].rearrange("p a b -> p (a b)").rearrange("p (c h s d) -> p c h s d", c=4, s=128 // HD if l1 else 4, d=HD)
                part = lambda s: v[:, :, :, s, :]
            else:
                v = stk[:].rearrange("p a b -> p (a b)").rearrange("p (h s d) -> p h s d", h=H, d=HD)
                part = lambda s: v[:, :, s, :]
            hi = part if queries else (lambda s: part(2 * s))
            lo = (lambda s: part(2 + s)) if queries else (lambda s: part(2 * s + 1))
            for s in range(2):
                a = self.copy_a(hi(s), src, f, R.get("stk"))
            yield
            b0 = self.tt(lo(0), src, hi(0).bitcast(F32), ALU.subtract, a)
            b1 = self.tt(lo(1), src, hi(0).bitcast(F32), ALU.subtract, a, eng=None if l1 else G)
            yield
            marks = []
            z = tbank
            for k in range(4):
                for i in range(4):
                    m = self.transpose(z[:, 128 * i:128 * i + 128], stk[:, 4 * k + i, :].bitcast(F32), b0, b1, *z.free, mark=i == 3)
                src4 = z[:].rearrange("p (h n) -> p h n", h=4)[:, :, 0:n]
                g = (self.copy_a if k % 2 else self.copy_v)(dst(k), src4, m, *free)
                z.free = [g]
                marks.append(g)
                yield
            R["stk"] = m
            return marks, [b0, b1]

        def drain(g):
            for _ in g:
                pass

        def stack_q(t):
            j = t % 2
            q = XF[:, :, 128 * t:128 * t + 128].rearrange("p c (h d) -> p c h d", d=HD)
            R["q", t], _ = yield from stack(R["qn", t], q, True, lambda k: qT[:, j, 4 * k:4 * k + 4, :], 128, old("Sq", t - 2))

        def stack_k(t):
            b, i = t // 2, t % 2
            n = 112 if l1 and i else 128
            dst = kT[b % 2]
            marks, R["kd", t] = yield from stack(
                R["kn", t], wide(cbk[t % 2]), False, lambda k: dst[:, 4 * k:4 * k + 4, 128 * i:128 * i + n], n,
                old("S", b - 2), *R.get("over", []))
            if l1 and i:
                marks.append(self.copy_a(dst[:, :, 240:256], kdT[:, :, 16 * b:16 * b + 16].bitcast(F32), *R["kdca"]))
            R["k", b] = R.get(("k", b), []) + marks

        def dca():
            z, cb = pbank, cbk[0]
            m = yield from project(lambda c: wd[:, c, 512:1024], [cd[:, c, :] for c in range(2)], md, mc)
            z.free = [self.tt(Vd[:], z[:], bd[:, 512:1024], ALU.add, m, mb)]
            R["vd"] = z.free[0]
            m = yield from project(lambda c: wd[:, c, 0:512], [cd[:, c, :] for c in range(2)], cen)
            f = self.tt(cb[:], z[:], bd[:, 0:512], ALU.add, m)
            g = f
            f = yield from square(cb[:], z, f, 2)
            f = scale(wide(cb), vec["kn_dca_w"], vec["kn_dca_b"], f, 2)
            R["kdca"], R["kd", -2] = yield from stack(f, wide(cb), False, lambda k: kdT[:, 4 * k:4 * k + 4, :], 128)
            R["over"] = [g]

        if not l1:
            cleared = G.do(lambda e: e.memset(VV[:], 0.0))

        steps = [(t, p) for t in range(NT) for p in range(NP_)]
        n = len(steps)
        heads = lambda p: (2 * p, 2 * p + 1) if l1 else (4 * (p // 2) + p % 2, 4 * (p // 2) + p % 2 + 2)
        sbk, tbk, obk, ybk = self.banks[2:4], self.banks[4:6], self.banks[6], self.banks[7]
        parts = ((0, 240), (240, 256)) if l1 else ((0, 256),)
        w = 2 * len(parts)

        def scores(s):
            t, p = steps[s]
            b, j = t // 2, s % 3
            z = sbk[s % 2]
            for i, h in enumerate(heads(p)):
                if l1:
                    l, r = qT[:, t % 2, h, :], kT[b % 2][:, h, :]
                else:
                    rows = slice(64 * (h % 2), 64 * (h % 2) + 64)
                    l, r = qT[rows, t % 2, h // 2, :], kT[b % 2][rows, h // 2, :]
                m = self.mm(z[:, 256 * i:256 * i + 256], [(l, r)], *R["q", t], *R["k", b], *z.free, mark=i == 1)
            R["s", s] = m
            if p == NP_ - 1:
                R["Sq", t] = m
                if t % 2:
                    R["S", b] = m

        def soften(s):
            t, p = steps[s]
            j = s % np_
            z, P, m = sbk[s % 2], Pb[j], R["s", s]
            zz = z[:].rearrange("p (h n) -> p h n", h=2)
            for k, (a, e) in enumerate(parts):
                f = self.red(mx[:, j, 2 * k:2 * k + 2], zz[:, :, a:e], ALU.max, m, R.get(("nb", s - np_)), negate=True)
            f = self.ts(nb[:, j, 0:w], mx[:, j, 0:w], SC, None, ALU.mult, None, f, R.get(("E", s - np_)))
            R["nb", s] = f
            for k, (a, e) in enumerate(parts):
                for i in range(2):
                    g = self.act(P[:, i, a:e], zz[:, i, a:e], ACT.Exp, f, R.get(("T", s - np_)), R.get(("N", s - np_)), xn_free,
                                 bias=nb[:, j, 2 * k + i:2 * k + i + 1], scale=SC, accum_out=sm[:, j, 2 * k + i:2 * k + i + 1])
            z.free = [g]
            R["E", s] = g

        def norm(s):
            j = s % np_
            r = V.do(lambda e: e.reciprocal(rc[:, j, 0:w], sm[:, j, 0:w]), R["E", s], R.get(("N", s - np_)))
            for k, (a, e) in enumerate(parts):
                g = self.tt(Pb[j][:, :, a:e], Pb[j][:, :, a:e], rc[:, j, 2 * k:2 * k + 2].unsqueeze(2).to_broadcast([128, 2, e - a]),
                            ALU.mult, r, eng=G)
            R["N", s] = g

        def turn_p(s):
            j = s % 2
            z, P = tbk[j], Pb[s % np_]
            for kt in range(2):
                for i in range(2):
                    k = 2 * kt + i
                    m = self.transpose(z[:, 128 * k:128 * k + 128], P[:, i, 128 * kt:128 * kt + 128], R["N", s], *z.free,
                                       mark=k == 3)
            R["T", s] = m
            f = (self.copy_a if l1 or s % 3 == 0 else self.copy_v)(PT[:, j, :, :].rearrange("p a n -> p (a n)"), z[:], m,
                                                                   R.get(("pv", s - 2)))
            z.free = [f]
            R["pt", s] = f

        def pv(s):
            t, p = steps[s]
            b, j = t // 2, s % 2
            z = obk
            for i, h in enumerate(heads(p)):
                r = 32 * (h if l1 else h // 2)
                first, last = (True, True) if l1 else (h % 2 == 0, h % 2 == 1)
                m = self.mm(z[r % 128:r % 128 + 32, r // 128 * 128:r // 128 * 128 + 128],
                            [(VV[:, b % 2, kt, 32 * h:32 * h + 32], PT[:, j, 2 * kt + i, :]) for kt in range(2)],
                            R["pt", s], R["v", b, 0], R["v", b, 1], *z.free, mark=i == 1, start=first, stop=last, skip=not l1)
            R["pv", s] = m
            if p == NP_ - 1:
                if t % 2:
                    R["O", b] = m
                f = self.copy_a(OT[:].rearrange("p c n -> p (c n)"), z[:], m, R.get("y"))
                z.free = [f]
                R["oT"] = f

        def outp(t, c):
            z = ybk
            m = self.mm(z[:], [(OT[:, c, :], wo[:, c, :])], R["oT"], mo, *z.free, mark=c == 3, start=c == 0, stop=c == 3)
            R["y"] = R["y", t] = m

        def add(t):
            z = ybk
            x = self.X[:, t, :]
            f = self.tt(x, x, z[:], ALU.add, R["y", t], self.xtok[t])
            z.free = [f]
            self.xtok[t] = self.tt(x, x, bo[:], ALU.add, f, mbo, eng=G)

        def ahead_a(t):
            if t + 2 < NT:
                yield from norm_q(t + 2)
            if t + 3 < NT:
                yield from norm_k(t + 3)
            if t + 2 < NT:
                yield from values(t + 2)

        def ahead_b(t):
            if t + 1 < NT:
                yield from stack_q(t + 1)
            if t + 2 < NT:
                yield from stack_k(t + 2)

        if l1:
            drain(dca())
        for g in (norm_q(0), norm_k(0), stack_q(0), norm_k(1), stack_k(0), norm_q(1), stack_k(1), norm_k(2), values(0), values(1)):
            drain(g)
        preps = []
        pieces = (17, 13) if l1 else (11, 13)
        for s in range(-depth, n + 1):
            u = s + depth
            if u < n and u % NP_ == 0:
                for g in preps:
                    drain(g)
                preps = [ahead_a(u // NP_), ahead_b(u // NP_)]
            q = u % NP_
            due = [c * (q + 1) // (NP_ - 1) - c * q // (NP_ - 1) for c in pieces]

            def advance(i):
                if preps and due[i] > 0:
                    due[i] -= 1
                    next(preps[i], None)

            for step in "SPTBAFONABA" if l1 else "TSPBFONABAA":
                if step == "T" and 0 <= s < n:
                    turn_p(s)
                if step == "B":
                    advance(1)
                if step == "A":
                    advance(0)
                if step == "S" and u < n:
                    scores(u)
                if step == "F" and u < n:
                    soften(u)
                if step == "N" and 0 <= s + 2 < n:
                    norm(s + 2)
                if step == "P" and s >= 1:
                    pv(s - 1)
                if step == "O" and s >= 1:
                    t, p = steps[s] if s < n else (NT, 0)
                    if t >= 1 and 1 <= p <= 4:
                        outp(t - 1, p - 1)
                    if t >= 1 and p == 5:
                        add(t - 1)
                    if t >= 1 and p == 7:
                        self.stat(t - 1)
        for c in range(4):
            outp(NT - 1, c)
        add(NT - 1)
        self.stat(NT - 1)

    def attend_l1(self):
        self.attend_narrow(1)

    def attend_l2(self):
        self.attend_narrow(2)

    def experts(self):
        A, V, G, PE, SP = self.A, self.V, self.G, self.PE, self.SP
        self.fence()
        base = self.top
        WB = self.at("WB", [128, 3 * 6144], F32, base)
        XN = self.at("XN", [128, NT, D], F32, base + 49152)
        self.top = base + 81920
        rl = self.sb("erl", [128, 4, 8], F32)
        rsc = self.sb("ersc", [128, 4], F32)
        rh, rlo = (self.sb(n, [128, 4, 8], F32R) for n in ("erh", "erlo"))
        esc = self.sb("eesc", [128, 8], F32)
        LG = self.sb("eLG", [128, NT, 8], F32)
        m8 = self.sb("em8", [128, NT, 8], F32)
        i8 = self.sb("ei8", [128, NT, 8], U32)
        oh = self.sb("eoh", [128, 2, NT, 8], F32)
        OA = self.sb("eOA", [128, NT, 8], F32)
        cu = self.sb("ecu", [128, 2, NT, 8], F32)
        pos = self.sb("epos", [128, NT, 8], F32)
        tm = self.sb("etm", [128, NT, 8], F32)
        i8f = self.sb("ei8f", [128, 8], F32)
        sm = self.sb("esm", [128, 12, NT], F32)
        POS = self.sb("ePOS", [128, 2, NT], I32)
        e8 = self.sb("ee8", [128, 6, 8], F32)
        n8 = self.sb("en8", [128, 8], I32)
        jio = self.sb("ejio", [1, 40], F32)
        ge = self.at("ege", [1, 40, 8], F32, self.xl_at + 30720)
        eb = self.sb("eeb", [1, 8, 40], F32)
        EI = self.sb("eEI", [1, 4, 40], I32)
        up = [self.xh_at]

        def work(name, shape, dt):
            t = self.at(name, shape, dt, up[0])
            up[0] += -(-int(np.prod(shape[1:])) * mybir.dt.size(dt) // 32) * 32
            assert up[0] <= self.xl_at + 30720
            return t

        xs = work("exs", [128, 3, 512], F32)
        xsT = work("exsT", [128, 2, 4, 128], F32)
        gl = work("egl", [128, 512], F32)
        hh = work("ehh", [128, 2, 512], F32)
        hT = work("ehT", [128, 2, 4, 128], F32)
        os_ = work("eos", [128, 2, 512], F32)
        gt = work("egt", [128, 2, 2, 512], F32)
        tri = work("etri", [128, 128], F32)

        m1 = self.load("raw0", rl[:], self.ins["L0_ffn_router_logits"])
        m2 = self.load("raw1", rsc[:], self.ins["L0_ffn_router_scale"])
        m3 = self.bcast("bias", esc[:], self.ins["L0_ffn_per_expert_scale"])
        f = self.tt(rl[:], rl[:], rsc[:].unsqueeze(2).to_broadcast([128, 4, 8]), ALU.mult, m1, m2)
        rw = self.split_w(rl[:], rh[:], rlo[:], f)
        a = G.do(lambda e: e.iota(i8f[:], [[1, 8]], base=0, channel_multiplier=0, allow_small_or_imprecise_dtypes=True))
        b = G.do(lambda e: e.iota(jio[:], [[1, 40]], base=0, channel_multiplier=0, allow_small_or_imprecise_dtypes=True))
        consts = b
        sq = [None, None]

        def square(t, d):
            sq[t % 2] = self.act(self.banks[6 + t % 2][:], XN[:, t, :], ACT.Square, d, sq[t % 2], accum_out=sm[:, 0, t:t + 1])

        self.ln_all(keep=XN, after=square)
        s = sq[(NT - 1) % 2]
        s = self.ts(sm[:, 1, :], sm[:, 0, :], 1.0 / 512, 1e-6, ALU.mult, ALU.add, s)
        s = self.rsqrt(sm[:, 2, :], sm[:, 1, :], s)
        s = self.ts(sm[:, 2, :], sm[:, 2, :], 512.0 ** -0.5, None, ALU.mult, None, s)
        for t in range(NT):
            z = self.banks[2 + t % 2]
            tok = slice(128 * t, 128 * t + 128)
            terms = []
            for c in range(4):
                xh, xl = self.XH[:, c, tok], self.XL[:, c, tok]
                terms += [(xh, rh[:, c, :]), (xh, rlo[:, c, :]), (xl, rh[:, c, :])]
            m = self.mm(z[:, 0:8], terms, rw, self.xnt[t], *z.free, mark=True)
            f = self.ts(LG[:, t, :], z[:, 0:8], sm[:, 2, t:t + 1], None, ALU.mult, None, m, s)
            z.free = [f]
            f = V.do(lambda e, t=t: e.max(m8[:, t, :], LG[:, t, :]), f)
            f = V.do(lambda e, t=t: e.max_index(i8[:, t, :], m8[:, t, :], LG[:, t, :]), f)
        logits = m
        g = self.tt(sm[:, 3, :], m8[:, :, 1], m8[:, :, 0], ALU.subtract, f)
        g = self.act(sm[:, 4, :], sm[:, 3, :], ACT.Exp, g)
        g = self.ts(sm[:, 5, :], sm[:, 4, :], 1.0, None, ALU.add, None, g)
        g = V.do(lambda e: e.reciprocal(sm[:, 6, :], sm[:, 5, :]), g)
        wts = self.tt(sm[:, 7, :], sm[:, 4, :], sm[:, 6, :], ALU.mult, g)
        for k in range(2):
            f = self.copy_v(sm[:, 8 + k, :], i8[:, :, k], f)
        for k in range(2):
            g = self.tt(oh[:, k, :, :], i8f[:].unsqueeze(1).to_broadcast([128, NT, 8]),
                        sm[:, 8 + k, :].unsqueeze(2).to_broadcast([128, NT, 8]), ALU.is_equal, f, consts)
        g = self.tt(OA[:], oh[:, 0, :, :], oh[:, 1, :, :], ALU.add, g)
        c1 = G.do(lambda e: e.memset(tri[:], 1.0), logits)
        c1 = G.do(lambda e: e.affine_select(out=tri[:], in_=tri[:], compare_op=ALU.is_gt, fill=0.0, base=0,
                                            pattern=[[1, 128]], channel_multiplier=-1), c1)
        z = self.banks[2]
        oa = OA[:].rearrange("p t e -> p (t e)")
        self.mm(z[:, 0:128], [(tri[:], oa)], g, c1, *z.free)
        m = self.mm(z[:, 128:256], [(self.ones[:], oa)], mark=True)
        pre = z[:, 0:128].rearrange("p (t e) -> p t e", t=NT)
        tot = z[:, 128:256].rearrange("p (t e) -> p t e", t=NT)
        f = self.copy_v(cu[:, 0, :, :], tot, m)
        j = 0
        for k in (1, 2, 4, 8):
            self.copy_v(cu[:, 1 - j, 0:k, :], cu[:, j, 0:k, :], f)
            f = self.tt(cu[:, 1 - j, k:NT, :], cu[:, j, k:NT, :], cu[:, j, 0:NT - k, :], ALU.add)
            j = 1 - j
        cum = cu[:, j, :, :]
        g = self.ts(n8[:], cum[:, NT - 1, :], 127.0, None, ALU.add, None, f)
        g = V.do(lambda e: e.tensor_scalar(n8[:], n8[:], 7, None, ALU.arith_shift_right), g)
        g = nblk = self.copy_v(e8[:, 0, :], n8[:], g)
        i = 0
        for k in (1, 2, 4):
            self.copy_v(e8[:, i + 1, 0:k], e8[:, i, 0:k], g)
            g = self.tt(e8[:, i + 1, k:8], e8[:, i, k:8], e8[:, i, 0:8 - k], ALU.add)
            i += 1
        ends = e8[:, 3, :]
        s = self.tt(e8[:, 4, :], ends, e8[:, 0, :], ALU.subtract, g)
        s = self.ts(e8[:, 4, :], e8[:, 4, :], 128.0, None, ALU.mult, None, s)
        f = self.tt(pos[:], pre, cum, ALU.add, f)
        f = self.tt(pos[:], pos[:], tot, ALU.subtract, f)
        z.free = [f]
        f = self.tt(pos[:], pos[:], e8[:, 4, :].unsqueeze(1).to_broadcast([128, NT, 8]), ALU.add, f, s)
        last = f
        for k in range(2):
            q = self.tt(tm[:], oh[:, k, :, :], pos[:], ALU.mult, last)
            q = self.red(sm[:, 10, :], tm[:], ALU.add, q)
            last = self.copy_v(POS[:, k, :], sm[:, 10, :], q)
        placed = last
        for k in range(2):
            q = self.tt(tm[:], oh[:, k, :, :], esc[:].unsqueeze(1).to_broadcast([128, NT, 8]), ALU.mult, last, m3)
            q = self.red(sm[:, 11, :], tm[:], ALU.add, q)
            last = self.tt(sm[:, 6 + k, :], sm[:, 6 + k, :], sm[:, 11, :], ALU.mult, q, wts)
        wts = last
        r0 = lambda k: eb[:, k, :]
        g = self.tt(ge[:], jio[:].unsqueeze(2).to_broadcast([1, 40, 8]), ends[0:1, :].unsqueeze(1).to_broadcast([1, 40, 8]),
                    ALU.is_ge, g, consts, logits)
        g = self.red(r0(0), ge[:], ALU.add, g)
        g = self.ts(r0(0), r0(0), 7.0, None, ALU.min, None, g)
        a = V.do(lambda e: e.memset(r0(1)[:, 0:1], 0.0))
        b = V.do(lambda e: e.memset(r0(7), 0.0))
        g = self.tt(r0(1)[:, 1:40], r0(0)[:, 1:40], r0(0)[:, 0:39], ALU.not_equal, g)
        g = V.do(lambda e: e.tensor_tensor_scan(r0(2), r0(1), r0(7), 0.0, ALU.add, ALU.add), g, a, b)
        h = self.ts(r0(3), r0(2), 3.0, -3.0, ALU.is_ge, ALU.mult, g)
        h = self.ts(r0(4), r0(2), 6.0, -3.0, ALU.is_ge, ALU.mult, h)
        h = self.tt(r0(3), r0(3), r0(4), ALU.add, h)
        h = self.tt(r0(3), r0(3), r0(2), ALU.add, h)
        a = V.do(lambda e: e.memset(r0(1)[:, 0:1], 1.0), h)
        a = self.copy_v(EI[:, 0, :], r0(0), a)
        a = self.copy_v(EI[:, 1, :], r0(1), a)
        a = known = self.copy_v(EI[:, 2, :], r0(3), a)

        marks = []
        for t in range(NT):
            for k in range(2):
                m = self.ch("scatter").send(G, lambda e, t=t, k=k: e.indirect_dma_start(
                    self.XS, bass.IndirectOffsetOnAxis(POS[:, k, t:t + 1], 0), XN[:, t, :], None), placed, self.zeroed)
        scattered = m

        banks = self.banks
        R, reg = {}, {}

        def weights(j):
            SP.wait(known, R.get(("down", j - 3)), scattered if j == 2 else None)

            def f(e):
                ex = e.value_load(EI[0:1, 0, j:j + 1], min_val=0, max_val=7)
                ch = e.value_load(EI[0:1, 1, j:j + 1], min_val=0, max_val=1)
                bu = e.value_load(EI[0:1, 2, j:j + 1], min_val=0, max_val=2)
                return e.dma_start(WB[:, bass.ds(bu * 6144, 6144)], self.ins["moe_w"][bass.ds(ex * 128, 128), :], cond=ch)

            R["w", j] = self.ch(f"moew{j % 3}").send(SP, f)

        def rows(j):
            R["xs", j] = self.load(f"xs{j % 3}", xs[:, j % 3, :], self.XS[128 * j:128 * j + 128, :], scattered, R.get(("T", j - 3)))

        def turn(j):
            z = banks[j % 2]
            for c in range(4):
                m = self.transpose(z[:, 128 * c:128 * c + 128], xs[:, j % 3, 128 * c:128 * c + 128], R["xs", j], *z.free, mark=c == 3)
            R["T", j] = m
            f = self.copy_v(xsT[:, j % 2, :, :].rearrange("p c n -> p (c n)"), z[:], m, R.get(("up", j - 2)))
            z.free = [f]
            R["xt", j] = f

        def upper(j):
            PE.wait(known)

            def f(e):
                reg["b"] = e.value_load(EI[0:1, 2, j:j + 1], min_val=0, max_val=2)
            PE.ops.append(f)
            ms = []
            for half in range(2):
                z = banks[2 + half]
                PE.wait(R["xt", j], R["w", j], *z.free)
                for c in range(4):
                    o = 1024 * c + 512 * half
                    m = PE.do(lambda e, z=z, c=c, o=o: e.matmul(z[:], xsT[:, j % 2, c, :], WB[:, bass.ds(reg["b"] * 6144 + o, 512)],
                                                                start=c == 0, stop=c == 3), mark=c == 3)
                ms.append(m)
            R["up", j] = m
            f = self.act(gl[:], banks[2][:], ACT.Gelu_apprx_tanh, ms[0], R.get("gl"))
            banks[2].free = [f]
            f = self.tt(hh[:, j % 2, :], banks[3][:], gl[:], ALU.mult, f, ms[1], R.get(("Th", j - 2)))
            banks[3].free = [f]
            R["gl"] = f
            R["h", j] = f

        def mid(j):
            z = banks[4 + j % 2]
            for c in range(4):
                m = self.transpose(z[:, 128 * c:128 * c + 128], hh[:, j % 2, 128 * c:128 * c + 128], R["h", j], *z.free, mark=c == 3)
            R["Th", j] = m
            f = self.copy_v(hT[:, j % 2, :, :].rearrange("p c n -> p (c n)"), z[:], m, R.get(("down", j - 2)))
            z.free = [f]
            R["ht", j] = f

        def lower(j):
            z = banks[6 + j % 2]
            PE.wait(R["ht", j], *z.free)

            def f(e):
                reg["d"] = e.value_load(EI[0:1, 2, j:j + 1], min_val=0, max_val=2)
            PE.ops.append(f)
            for c in range(4):
                o = 4096 + 512 * c
                m = PE.do(lambda e, c=c, o=o: e.matmul(z[:], hT[:, j % 2, c, :], WB[:, bass.ds(reg["d"] * 6144 + o, 512)],
                                                       start=c == 0, stop=c == 3), mark=c == 3)
            R["down", j] = m
            f = self.copy_v(os_[:, j % 2, :], z[:], m, R.get(("out", j - 2)))
            z.free = [f]
            R["out", j] = self.load(f"os{j % 2}", self.OS[128 * j:128 * j + 128, :], os_[:, j % 2, :], f)

        weights(0)
        weights(1)
        rows(0)
        rows(1)
        weights(2)
        rows(2)
        turn(0)
        upper(0)
        for j in range(NBLK):
            if j + 1 < NBLK:
                turn(j + 1)
            mid(j)
            if j + 1 < NBLK:
                upper(j + 1)
            lower(j)
            if j + 3 < NBLK:
                weights(j + 3)
                rows(j + 3)
        outs = [R["out", NBLK - 2], R["out", NBLK - 1]]
        for t in range(NT):
            x = self.X[:, t, :]
            for k in range(2):
                m = self.ch(f"gather{k}{t % 2}").send(G, lambda e, t=t, k=k: e.indirect_dma_start(
                    gt[:, t % 2, k, :], None, self.OS, bass.IndirectOffsetOnAxis(POS[:, k, t:t + 1], 0)), *outs, R.get(("g", t - 2)), s)
                self.xtok[t] = self.stt(x, gt[:, t % 2, k, :], sm[:, 6 + k, t:t + 1], x, ALU.mult, ALU.add, m, wts, self.xtok[t])
            R["g", t] = self.xtok[t]
            self.stat(t)

    def finish(self):
        self.fence()
        o = self.out.rearrange("b (t p) d -> p (b t) d", p=128)
        for h in range(4):
            m = self.load("out", o[:, 4 * h:4 * h + 4, :], self.X[:, 4 * h:4 * h + 4, :], *self.xtok[4 * h:4 * h + 4])
        self.SP.wait(m)

    def build(self):
        self.start()
        for p in self.phases:
            p(self)
        self.finish()
        with self.nc.Block() as block:
            block.tensor(self.PE.play)
            block.scalar(self.A.play)
            block.vector(self.V.play)
            block.gpsimd(self.G.play)
            block.sync(self.SP.play)


ALL = [lambda p: p.attend_wide(0), lambda p: p.experts(), lambda p: p.attend_l1(), lambda p: p.ternary_ffn(),
       lambda p: p.attend_l2(), lambda p: p.mix(), lambda p: p.attend_wide(3), lambda p: p.choice()]


def program(nc, ins, out, phases=ALL):
    Program(nc, ins, out, phases).build()


def lay_out(x):
    a = {k: np.asarray(v) for k, v in x.items()}

    def rows(w, n):
        return np.ascontiguousarray(w.reshape(n, 128, -1).transpose(1, 0, 2))

    out = {k: a[k] for k in ("x", "mask_BxS2_bf1", "fside_BxSx2_0", "L3_xattn_gq", "L3_xattn_gk",
                             "L0_ffn_per_expert_scale", "L3_ffn_router_b", "L3_ffn_expert_b",
                             "L1_xattn_bq", "L1_xattn_bk", "L1_xattn_bv", "L1_xattn_bkv_dca",
                             "L1_xattn_qn_w", "L1_xattn_qn_b", "L1_xattn_kn_w", "L1_xattn_kn_b",
                             "L1_xattn_kn_dca_w", "L1_xattn_kn_dca_b", "L1_xattn_bo", "L2_xattn_bout", "L2_ffn_bias")}
    out["mask_BxS2_bf1"] = a["mask_BxS2_bf1"].view(np.uint8)
    out["ctxT"] = rows(np.ascontiguousarray(a["ctx_1024"].reshape(T, C).T), 2)
    for L, kw in ((0, 128), (3, 256)):
        p = f"L{L}_xattn_"
        out[p + "Wq"] = a[p + "Wq"].reshape(4, 128, 8, 256).transpose(2, 1, 0, 3)
        for k in ("Wk", "Wv"):
            out[p + k] = a[p + k].reshape(2, 128, 8, kw).transpose(2, 1, 0, 3)
        out[p + "Wo"] = a[p + "Wo"].reshape(8, 2, 128, 512).transpose(0, 2, 1, 3)
    g = a["L0_ffn_gating_einsum"].transpose(0, 3, 1, 2).reshape(8, 4, 128, 1024).transpose(0, 2, 1, 3).reshape(8, 128, 4096)
    l = a["L0_ffn_linear"].reshape(8, 4, 128, 512).transpose(0, 2, 1, 3).reshape(8, 128, 2048)
    out["moe_w"] = np.concatenate([g, l], axis=2).reshape(8 * 128, 6144)
    out["L0_ffn_router_logits"] = rows(a["L0_ffn_router_logits"], 4)
    out["L0_ffn_router_scale"] = a["L0_ffn_router_scale"].reshape(4, 128).T
    out["L1_xattn_Wq"] = rows(a["L1_xattn_Wq"], 4)
    out["L1_xattn_Wkv"] = rows(np.concatenate([a["L1_xattn_Wk"], a["L1_xattn_Wv"]], axis=1), 2)
    out["L1_xattn_Wkv_dca"] = rows(a["L1_xattn_Wkv_dca"], 2)
    out["L1_xattn_Wo"] = rows(a["L1_xattn_Wo"], 4)
    out["ctx_dcaT"] = rows(np.ascontiguousarray(a["ctx_1024"][:, -16:, :].reshape(128, C).T), 2)
    for k in ("W_up", "W_gate"):
        out["L1_ffn_" + k] = a["L1_ffn_" + k].T.reshape(4, 128, 4, 512).transpose(2, 1, 0, 3)
    out["L1_ffn_W_down"] = a["L1_ffn_W_down"].T.reshape(4, 4, 128, 512).transpose(0, 2, 1, 3)
    out["L2_xattn_Wq"] = rows(a["L2_xattn_Wq"], 4)
    out["L2_xattn_Wkv"] = rows(a["L2_xattn_Wkv"], 2)
    out["L2_xattn_Wout"] = rows(a["L2_xattn_Wout"], 4)
    out["L2_ffn_factors"] = a["L2_ffn_factors"].reshape(8, 4, 128, 512).transpose(0, 2, 1, 3)
    out["L3_ffn_router_w"] = rows(a["L3_ffn_router_w"], 4)
    out["L3_ffn_expert_w"] = rows(a["L3_ffn_expert_w"], 4)
    return {k: np.ascontiguousarray(v) for k, v in out.items()}


def kernel(**inputs):
    import concourse.bacc as _bacc
    from concourse.bass_utils import run_bass_kernel_spmd as _run

    nc = _bacc.Bacc("TRN2", target_bir_lowering=False, num_devices=1)
    arrays = lay_out(inputs)
    ins = {k: nc.dram_tensor("in_" + k, v.shape, mybir.dt.from_np(v.dtype), kind="ExternalInput").ap() for k, v in arrays.items()}
    out = nc.dram_tensor("out_0", (NB, S, D), F32, kind="ExternalOutput").ap()
    program(nc, ins, out)
    r = _run(nc, [{"in_" + k: v for k, v in arrays.items()}], core_ids=[0])
    return r.results[0]["out_0"]
```

```python
import concourse.bass as bass
from concourse import mybir
from concourse.alu_op_type import AluOpType as ALU
import numpy as np

ACT = mybir.ActivationFunctionType
AX = mybir.AxisListType
F32 = mybir.dt.float32
F32R = mybir.dt.float32r
BF16 = mybir.dt.bfloat16
I32 = mybir.dt.int32
U32 = mybir.dt.uint32
U8 = mybir.dt.uint8

NB, S, D, C = 8, 256, 512, 256
T = NB * S
NT = T // 128
NBLK = 39
BASE = 16512
END = 229344


class Engine:

    def __init__(self, sem):
        self.sem, self.n, self.ops, self.seen = sem, 0, [], {}

    def wait(self, *marks):
        for m in marks:
            if m is None:
                continue
            sem, value = m
            if self.seen.get(sem.name, 0) < value:
                self.seen[sem.name] = value
                self.ops.append(lambda e, s=sem, v=value: e.wait_ge(s, v))

    def do(self, f, *waits, mark=True):
        self.wait(*waits)
        if not mark:
            self.ops.append(f)
            return None
        self.n += 1
        self.ops.append(lambda e: f(e).then_inc(self.sem, 1))
        return (self.sem, self.n)

    @property
    def last(self):
        return (self.sem, self.n) if self.n else None

    def play(self, e):
        for f in self.ops:
            f(e)


class Channel:

    def __init__(self, sem):
        self.sem, self.n = sem, 0

    def send(self, eng, f, *waits):
        eng.wait(*waits)
        self.n += 16
        eng.ops.append(lambda e: f(e).then_inc(self.sem, 16))
        return (self.sem, self.n)


class Bank:
    def __init__(self, t):
        self.t, self.free = t, []

    def __getitem__(self, k):
        return self.t[k]


class Program:
    def __init__(self, nc, ins, out, phases):
        self.nc, self.ins, self.out = nc, ins, out
        self.names = 0
        self.PE, self.A, self.V, self.G, self.SP = (Engine(self.sem(n)) for n in ("s_pe", "s_act", "s_dve", "s_pool", "s_sp"))
        self.engines = [self.PE, self.A, self.V, self.G, self.SP]
        self.channels = {}
        self.banks = [Bank(nc.alloc_psum_tensor(f"bank{i}", [128, 512], F32)) for i in range(8)]
        self.top = BASE
        self.X = self.sb("X", [128, NT, D], F32)
        self.XH = self.sb("XH", [128, 4, T], F32R)
        self.XL = self.sb("XL", [128, 4, T], F32R)
        self.xh_at, self.xl_at = BASE + 32768, BASE + 65536
        self.CTX = self.sb("CTX", [128, 2, T], F32)
        self.ident = self.sb("ident", [128, 128], F32)
        self.ones = self.sb("ones", [128, 128], F32)
        self.mhalf = self.sb("mhalf", [128, 64], F32)
        self.zero = self.sb("zero", [128, 128], F32)
        self.mv = self.sb("mv", [128, NT, 2], F32)
        self.rs = self.sb("rs", [128, NT], F32)
        self.st = self.sb("st", [128, NT, 6], F32)
        self.xn_at = self.top
        self.xn = self.sb("xn", [128, 2, D], F32)
        self.sc1 = self.sb("sc1", [128, 16], F32)
        self.s12 = self.sb("s12", [128, 12], F32)
        self.sizes = self.early = None
        self.XF = self.at("XF", [128, 4, T], F32, self.xh_at)
        self.arena = self.top
        self.xtok = [None] * NT
        self.phases = phases

    def sem(self, name):
        return self.nc.alloc_semaphore(name)

    def ch(self, name):
        if name not in self.channels:
            self.channels[name] = Channel(self.sem("d_" + name))
        return self.channels[name]

    def at(self, name, shape, dt, offset):
        self.names += 1
        return self.nc.alloc_sbuf_tensor_at(f"{name}_{self.names}", shape, dt, offset=offset)

    def sb(self, name, shape, dt):
        size = int(np.prod(shape[1:])) * mybir.dt.size(dt)
        t = self.at(name, shape, dt, self.top)
        self.top += -(-size // 32) * 32
        assert self.top <= END, (name, self.top - END)
        return t

    def fence(self):
        marks = [e.last for e in self.engines] + [(c.sem, c.n) for c in self.channels.values() if c.n]
        for e in self.engines:
            e.wait(*marks)
        self.top = self.arena
        for b in self.banks:
            b.free = []

    def mm(self, out, terms, *waits, mark=False, start=True, stop=True, skip=False):
        self.PE.wait(*waits)
        n = len(terms)
        for i, (l, r) in enumerate(terms):
            m = self.PE.do(
                lambda e, l=l, r=r, a=start and i == 0, z=stop and i == n - 1: e.matmul(
                    out, l, r, start=a, stop=z, skip_group_check=skip),
                mark=mark and i == n - 1)
        return m

    def transpose(self, out, in_, *waits, mark=False):
        return self.PE.do(lambda e: e.transpose(out, in_, self.ident[0:in_.shape[0], 0:in_.shape[0]]), *waits, mark=mark)

    def act(self, out, in_, func, *waits, **kw):
        return self.A.do(lambda e: e.activation(out, in_, func, **kw), *waits)

    def copy_a(self, out, in_, *waits):
        return self.act(out, in_, ACT.Copy, *waits)

    def copy_v(self, out, in_, *waits):
        return self.V.do(lambda e: e.tensor_copy(out, in_), *waits)

    def tt(self, out, a, b, op, *waits, eng=None):
        return (eng or self.V).do(lambda e: e.tensor_tensor(out, a, b, op), *waits)

    def ts(self, out, a, s1, s2, op0, op1, *waits, eng=None):
        if s2 is None:
            return (eng or self.V).do(lambda e: e.tensor_scalar(out, a, s1, None, op0), *waits)
        return (eng or self.V).do(lambda e: e.tensor_scalar(out, a, s1, s2, op0, op1), *waits)

    def stt(self, out, a, s, b, op0, op1, *waits):
        return self.V.do(lambda e: e.scalar_tensor_tensor(out, a, s, b, op0, op1), *waits)

    def red(self, out, a, op, *waits, **kw):
        return self.V.do(lambda e: e.tensor_reduce(out, a, AX.X, op, **kw), *waits)

    def rsqrt(self, out, a, *waits):
        n = a.shape[1]
        return self.tt(out, a, self.mhalf[0:a.shape[0], 0:n], ALU.pow, *waits, eng=self.G)

    def load(self, name, out, in_, *waits):
        return self.ch(name).send(self.SP, lambda e: e.dma_start(out, in_), *waits)

    def start(self):
        G, V = self.G, self.V
        a = G.do(lambda e: e.memset(self.ident[:], 0.0))
        b = G.do(lambda e: e.affine_select(out=self.ident[:], in_=self.ident[:], compare_op=ALU.not_equal, fill=1.0,
                                           base=0, pattern=[[-1, 128]], channel_multiplier=1), a)
        c = G.do(lambda e: e.memset(self.mhalf[:], -0.5))
        z = G.do(lambda e: e.memset(self.zero[:], 0.0))
        d = V.do(lambda e: e.memset(self.ones[:], 1.0))
        x = self.ins["x"].rearrange("b (t p) d -> p (b t) d", p=128)
        for h in range(4):
            m = self.load(f"x{h}", self.X[:, 4 * h:4 * h + 4, :], x[:, 4 * h:4 * h + 4, :])
            self.xtok[4 * h:4 * h + 4] = [m] * 4
        for t in range(NT):
            self.stat(t)
        m = self.load("ctx", self.CTX[:], self.ins["ctxT"])
        for e in self.engines:
            e.wait(a, b, c, d)
        self.ctxtok = m
        self.XS = self.nc.dram_tensor("rows_in", (NBLK * 128, D), F32, kind="Internal").ap()
        self.OS = self.nc.dram_tensor("rows_out", (NBLK * 128, D), F32, kind="Internal").ap()
        self.zeros, self.cleared = z, 0
        self.FS = self.nc.dram_tensor("factor_sum", (128, 4, D), F32, kind="Internal").ap()
        self.factors = self.coming = None

    def clear(self):
        q = self.cleared
        self.cleared += 1
        self.zeroed = self.load("zero", self.XS.rearrange("(j p) d -> p j d", p=128)[:, :, 128 * q:128 * q + 128],
                                self.zero[:].unsqueeze(1).to_broadcast([128, NBLK, 128]), self.zeros)

    def stat(self, t):
        V = self.V
        a = V.do(lambda e: e.bn_stats(self.st[:, t, :], self.X[:, t, :]), self.xtok[t])
        self.stats = V.do(lambda e: e.bn_aggr(self.mv[:, t, :], self.st[:, t, :]), a)

    def ln_all(self, **kw):
        for _ in self.ln_rest(**kw):
            pass
        return self.turned

    def ln_rest(self, **kw):
        steps, self.early = self.early or self.ln_steps(**kw), None
        return steps

    def ln_steps(self, keep=None, plain=None, after=None, each=False):
        if not each:
            a = self.ts(self.sc1[:], self.mv[:, :, 1], 1e-5, None, ALU.add, None, self.stats)
            a = self.rsqrt(self.rs[:], self.sc1[:], a)
        self.xnt, ready, turned = [None] * NT, [None] * NT, [None] * NT

        def norm(t):
            xn = self.xn[:, t % 2, :] if keep is None else keep[:, t, :]
            if each:
                r = self.ts(self.sc1[:, t:t + 1], self.mv[:, t, 1:2], 1e-5, None, ALU.add, None, self.stats)
                r = self.rsqrt(self.rs[:, t:t + 1], self.sc1[:, t:t + 1], r)
            else:
                r = a
            ready[t] = self.ts(xn, self.X[:, t, :], self.mv[:, t, 0:1], self.rs[:, t:t + 1], ALU.subtract, ALU.mult,
                               r, self.xtok[t], turned[t - 2] if t >= 2 and keep is None else None)

        def turn(t):
            xn = self.xn[:, t % 2, :] if keep is None else keep[:, t, :]
            bank = self.banks[t % 2]
            tok = slice(128 * t, 128 * t + 128)
            for k in range(4):
                p = self.transpose(bank[:, 128 * k:128 * k + 128], xn[:, 128 * k:128 * k + 128], ready[t], *bank.free, mark=k == 3)
            turned[t] = p
            src = bank[:].rearrange("p (c n) -> p c n", c=4)
            if plain is not None:
                f = (self.copy_a if t % 2 or each else self.copy_v)(plain[:, :, tok], src, p)
            else:
                f = self.copy_a(self.XH[:, :, tok], src, p)
                f = self.tt(self.XL[:, :, tok], src, self.XH[:, :, tok].bitcast(F32), ALU.subtract, f)
            bank.free = [f]
            self.xnt[t] = f

        norm(0)
        for t in range(NT):
            if t + 1 < NT:
                norm(t + 1)
            turn(t)
            if after is not None:
                after(t, ready[t])
            self.turned = turned[t]
            yield t

    def route(self, n, hi, lo, turned, w, **kw):
        def group(k):
            z = self.banks[4 + k % 2]
            tok = slice(512 * k, 512 * k + 512)
            terms = []
            for c in range(4):
                xh, xl = self.XH[:, c, tok], self.XL[:, c, tok]
                terms += [(hi[:, c, :], xh), (hi[:, c, :], xl), (lo[:, c, :], xh)]
            m = self.mm(z[0:n, :], terms, w, *self.xnt[4 * k:4 * k + 4], *z.free, mark=True)
            f = self.copy_a(turned[:, tok], z[0:n, :], m)
            z.free = [f]
            return f

        k = 0
        for t in self.ln_rest(**kw):
            if t >= 4 * k + 5:
                group(k)
                k += 1
        while k < 4:
            f = group(k)
            k += 1
        z = self.banks[2]
        for t in range(NT):
            m = self.transpose(z[:, n * t:n * t + n], turned[:, 128 * t:128 * t + 128], f, *z.free, mark=t == NT - 1)
        return z[:, 0:n * NT].rearrange("p (t e) -> p t e", t=NT), m

    def attend_wide(self, L):
        A, V, G, PE = self.A, self.V, self.G, self.PE
        l0 = L == 0
        kh = 1 if l0 else 2
        kw = 128 * kh
        self.fence()
        lns = self.ln_rest()
        wqr = self.sb("wqr", [128, 4, 256], F32)
        wor = self.sb("wor", [128, 2, 512], F32)
        wk = self.sb("wk", [128, 2, 2, kw], F32)
        wv = self.sb("wv", [128, 2, 2, kw], F32)
        wqh, wql = (self.sb(n, [128, 2, 4, 256], F32R) for n in ("wqh", "wql"))
        woh, wol = (self.sb(n, [128, 2, 2, 512], F32R) for n in ("woh", "wol"))
        QH, QL = (self.sb(n, [128, 2, 256], F32R) for n in ("QH", "QL"))
        KH, KL = (self.sb(n, [128, kh, 256], F32R) for n in ("KH", "KL"))
        VH, VL = (self.sb(n, [128, 2, 2, kw], F32R) for n in ("VH", "VL"))
        P = self.sb("P", [128, 2, 2, 256], F32)
        PH, PL = (self.sb(n, [128, 2, 2, 2, 128], F32R) for n in ("PH", "PL"))
        OH, OL = (self.sb(n, [128, 2, 256], F32R) for n in ("OH", "OL"))
        mx, nb, sm, rc = (self.sb(n, [128, 2, 4], F32) for n in ("mx", "nb", "sm", "rc"))
        pre = f"L{L}_xattn_"
        first = []
        if l0:
            onesb = self.sb("onesb", [1, 128], BF16)
            mu8 = self.sb("mu8", [128, T], U8)
            anym = self.sb("anym", [128, NB], F32)
            mrow = self.sb("mrow", [1, T], BF16)
            m = self.load("mask", mu8[:], self.ins["mask_BxS2_bf1"].rearrange("(a b) s -> a (b s)", a=1).to_broadcast([128, T]))
            a = self.red(anym[:], mu8[:].rearrange("p (b s) -> p b s", b=NB), ALU.max, m)
            b = self.ts(mrow[:], mu8[0:1, :], 1.0, 1e30, ALU.subtract, ALU.mult, m)
            c = V.do(lambda e: e.memset(onesb[:], 1.0))
            first = [a, b, c]
        else:
            gq = self.sb("gq", [128, 2], F32)
            m = self.load("gqk", gq[:, 0:1], self.ins["L3_xattn_gq"].rearrange("(p a) -> p a", a=1))
            m = self.load("gqk", gq[:, 1:2], self.ins["L3_xattn_gk"].rearrange("(p a) -> p a", a=1))
            gqk = self.sb("gqkp", [128, 1], F32)
            first = [self.tt(gqk[:], gq[:, 0:1], gq[:, 1:2], ALU.mult, m)]
            K1 = self.sb("K1", [128, 4, 128], F32)
            q2 = self.sb("q2", [128, 2, 256], F32)
            kst = self.sb("kst", [128, 3, 4], F32)
            qst = self.sb("qst", [128, 2, 4], F32)
        SC = 128.0 ** -0.5
        loaded, split = {}, {}
        done = {}

        def fetch(g):
            s, w = split.get(g - 1), done.get(("kv", g - 2))
            a = self.load("wq", wqr[:], self.ins[pre + "Wq"][g], s and s[0])
            b = self.load(f"wk{g % 2}", wk[:, g % 2, :, :], self.ins[pre + "Wk"][g], w)
            b = self.load(f"wk{g % 2}", wv[:, g % 2, :, :], self.ins[pre + "Wv"][g], w)
            c = self.load("wo", wor[:], self.ins[pre + "Wo"][g], s and s[1])
            loaded[g] = (a, b, c)
            if l0 and 2 <= g < 6:
                self.clear()

        def part(g):
            a, _, c = loaded[g]
            j = g % 2
            h = self.copy_a(wqh[:, j, :, :], wqr[:], a, done.get(("q", g - 2)))
            q = self.tt(wql[:, j, :, :], wqr[:], wqh[:, j, :, :].bitcast(F32), ALU.subtract, h)
            h = self.copy_a(woh[:, j, :, :], wor[:], c, done.get(("y", g - 2)))
            o = self.tt(wol[:, j, :, :], wor[:], woh[:, j, :, :].bitcast(F32), ALU.subtract, h)
            split[g] = (q, o)

        units = [(g, b) for g in range(8) for b in range(NB)]
        turn = [0]

        def bank_a():
            turn[0] += 1
            return self.banks[turn[0] % 2]

        sb_, tb, ob, yb = self.banks[2:4], self.banks[4:6], self.banks[6], self.banks[7]
        R = {}

        def proj(u):
            g, b = units[u]
            j, w = u % 2, g % 2
            if b == 0 and g + 1 < 8:
                fetch(g + 1)
            if b == 5 and g + 1 < 8:
                part(g + 1)
            if b == 0:
                R["xw"] = split[g][0]
            tok = slice(256 * b, 256 * b + 256)
            k = bank_a()
            if l0:
                m = self.mm(k[:, 0:256], [(wk[:, w, c, :], self.CTX[:, c, tok]) for c in range(2)],
                            self.ctxtok, loaded[g][1], *k.free)
                for i in range(2):
                    tk = slice(256 * b + 128 * i, 256 * b + 128 * i + 128)
                    m = self.mm(k[:, 256 + 128 * i:384 + 128 * i],
                                [(self.CTX[:, c, tk], wv[:, w, c, :]) for c in range(2)], mark=i == 1)
                f = self.copy_v(KH[:, 0, :], k[:, 0:256], m, R.get(("S", u - 1)))
                f = self.tt(KL[:, 0, :], k[:, 0:256], KH[:, 0, :].bitcast(F32), ALU.subtract, f)
                v = k[:, 256:512].rearrange("p (t n) -> p t n", t=2)
                f = self.copy_v(VH[:, j, :, :], v, R.get(("O", u - 2)))
                f = self.tt(VL[:, j, :, :], v, VH[:, j, :, :].bitcast(F32), ALU.subtract, f)
                k.free = [f]
                R["k", u] = f
            else:
                for i in range(2):
                    tk = slice(256 * b + 128 * i, 256 * b + 128 * i + 128)
                    m = self.mm(k[:, 256 * i:256 * i + 256], [(self.CTX[:, c, tk], wk[:, w, c, :]) for c in range(2)],
                                self.ctxtok, loaded[g][1], *k.free, mark=i == 1)
                sq = sb_[1]
                f = self.act(sq[:], k[:], ACT.Square, m, *sq.free)
                s = self.red(kst[:, 0, :], sq[:].rearrange("p (t n) -> p t n", t=4), ALU.add, f, R.get("kr"))
                sq.free = [s]
                s = self.ts(kst[:, 1, :], kst[:, 0, :], 1.0 / 128, 1e-5, ALU.mult, ALU.add, s)
                s = self.rsqrt(kst[:, 2, :], kst[:, 1, :], s)
                f = self.tt(K1[:], k[:].rearrange("p (t n) -> p t n", t=4),
                            kst[:, 2, :].unsqueeze(2).to_broadcast([128, 4, 128]), ALU.mult, s, R.get("kt"))
                R["kr"] = f
                k.free = [f]
                R["k1", u] = f
            z = bank_a()
            for h in range(2):
                cs = slice(128 * h, 128 * h + 128)
                terms = []
                for c in range(4):
                    xh, xl = self.XH[:, c, tok], self.XL[:, c, tok]
                    terms += [(wqh[:, w, c, cs], xh), (wqh[:, w, c, cs], xl), (wql[:, w, c, cs], xh)]
                m = self.mm(z[:, 256 * h:256 * h + 256], terms, self.xnt[2 * b], self.xnt[2 * b + 1], split[g][0],
                            *z.free, mark=h == 1)
            done[("q", g)] = mq = m
            zz = z[:].rearrange("p (h n) -> p h n", h=2)
            f = self.copy_a(QH[:], zz, mq, R.get(("S", u - 1)))
            if not l0:
                f = self.act(q2[:], zz, ACT.Square, m, R.get(("qs", u - 1)))
            l = self.tt(QL[:], zz, QH[:].bitcast(F32), ALU.subtract, f)
            z.free = [l]
            R["q2", u] = f
            R["q", u] = l
            if not l0:
                v = sb_[0]
                for i in range(2):
                    tk = slice(256 * b + 128 * i, 256 * b + 128 * i + 128)
                    m = self.mm(v[:, 256 * i:256 * i + 256], [(self.CTX[:, c, tk], wv[:, w, c, :]) for c in range(2)],
                                *v.free, mark=i == 1)
                vv = v[:].rearrange("p (t n) -> p t n", t=2)
                f = self.copy_a(VH[:, j, :, :], vv, m, R.get(("O", u - 2)))
                f = self.tt(VL[:, j, :, :], vv, VH[:, j, :, :].bitcast(F32), ALU.subtract, f)
                v.free = [f]
                R["v", u] = f
            done[("kv", g)] = self.PE.last

        def late(u):
            j = u % 2
            k = bank_a()
            for i in range(2):
                for h in range(2):
                    m = self.transpose(k[:, 256 * h + 128 * i:256 * h + 128 * i + 128], K1[:, 2 * i + h, :],
                                       R["k1", u], *k.free, mark=i + h == 2)
            R["kt"] = m
            kk = k[:].rearrange("p (h n) -> p h n", h=2)
            f = self.act(KH[:], kk, ACT.Copy, m, R.get(("S", u - 1)), *first, scale=gqk[:, 0:1])
            f = self.stt(KL[:], kk, gqk[:, 0:1], KH[:].bitcast(F32), ALU.mult, ALU.subtract, f)
            k.free = [f]
            R["k", u] = f
            z = bank_a()
            for qt in range(2):
                for h in range(2):
                    m = self.mm(z[:, 2 * qt + h:2 * qt + h + 1],
                                [(q2[:, h, 128 * qt:128 * qt + 128], self.ones[:, 0:1])], R["q2", u], *z.free,
                                mark=qt + h == 2)
            R["qs", u] = m
            f = self.ts(qst[:, 0, :], z[:, 0:4], 128e-5, None, ALU.add, None, m, R.get("qr"))
            z.free = [f]
            f = self.rsqrt(qst[:, 1, :], qst[:, 0, :], f, R.get(("E", u - 1)))
            R["qr"] = f

        def scores(u):
            g, b = units[u]
            j = u % 2
            for qt in range(2):
                z = sb_[qt]
                if l0:
                    mb = mrow[0:1, 256 * b:256 * b + 256].unsqueeze(1).to_broadcast([1, 2, 256])
                    self.mm(z[:].rearrange("p (h n) -> p h n", h=2), [(onesb[:], mb)], *first, *z.free, stop=False, skip=True)
                for h in range(2):
                    qh, ql = (x[:, h, 128 * qt:128 * qt + 128] for x in (QH, QL))
                    kh_, kl = (x[:, 0 if l0 else h, :] for x in (KH, KL))
                    m = self.mm(z[:, 256 * h:256 * h + 256], [(qh, kh_), (qh, kl), (ql, kh_)],
                                R["q", u], R["k", u], *z.free, start=not l0, skip=l0, mark=h == 1)
                c = slice(2 * qt, 2 * qt + 2)
                s = self.red(mx[:, j, c], z[:].rearrange("p (h n) -> p h n", h=2), ALU.max, m, R.get(("N", u - 2)), negate=True)
                if l0:
                    s = self.ts(nb[:, j, c], mx[:, j, c], SC, None, ALU.mult, None, s, R.get(("E", u - 2)))
                else:
                    s = self.tt(nb[:, j, c], mx[:, j, c], qst[:, 1, c], ALU.mult, s, R["qr"], R.get(("E", u - 2)))
                for h in range(2):
                    i = 2 * qt + h
                    f = self.act(P[:, qt, h, :], z[:, 256 * h:256 * h + 256], ACT.Exp, s, R.get(("T", u - 1)),
                                 R.get(("N", u - 2)), bias=nb[:, j, i:i + 1], scale=SC if l0 else qst[:, 1, i:i + 1],
                                 accum_out=sm[:, j, i:i + 1])
                z.free = [f]
            R["S", u] = m
            R["E", u] = f

        def norm(u):
            g, b = units[u]
            j = u % 2
            r = V.do(lambda e: e.reciprocal(rc[:, j, :], sm[:, j, :]), R["E", u])
            if l0:
                r = self.ts(rc[:, j, :], rc[:, j, :], anym[:, b:b + 1], None, ALU.mult, None, r)
            for qt in range(2):
                for h in range(2):
                    i = 2 * qt + h
                    r2 = self.ts(P[:, qt, h, :], P[:, qt, h, :], rc[:, j, i:i + 1], None, ALU.mult, None, r)
            R["N", u] = r2

        def turn_p(u):
            j = u % 2
            fs = []
            for qt in range(2):
                z = tb[qt]
                for kt in range(2):
                    for h in range(2):
                        i = 2 * kt + h
                        m = self.transpose(z[:, 128 * i:128 * i + 128], P[:, qt, h, 128 * kt:128 * kt + 128],
                                           R["N", u], *z.free, mark=i == 3)
                hi, lo = (x[:, qt, :, :, :].rearrange("p k h n -> p (k h n)") for x in (PH, PL))
                f = self.copy_a(hi, z[:], m, R.get(("O", u - 1)))
                f = self.tt(lo, z[:], hi.bitcast(F32), ALU.subtract, f)
                z.free = [f]
                fs.append(f)
            R["T", u] = m
            R["pt", u] = fs

        def pv_mm(u):
            j = u % 2
            z = ob
            for h in range(2):
                vs = slice(0, 128) if l0 else slice(128 * h, 128 * h + 128)
                terms = []
                for kt in range(2):
                    vh, vl, ph, pl = VH[:, j, kt, vs], VL[:, j, kt, vs], PH[:, :, kt, h, :], PL[:, :, kt, h, :]
                    terms += [(vh, ph), (vh, pl), (vl, ph)]
                m = self.mm(z[:, 256 * h:256 * h + 256].rearrange("p (q n) -> p q n", q=2), terms,
                            *R["pt", u], R["k" if l0 else "v", u], *z.free, mark=h == 1)
            R["O", u] = m

        def pv_out(u):
            z, m = ob, R["O", u]
            zz = z[:].rearrange("p (h n) -> p h n", h=2)
            f = self.copy_a(OH[:], zz, m, R.get(("Y", u - 1)))
            f = self.tt(OL[:], zz, OH[:].bitcast(F32), ALU.subtract, f)
            z.free = [f]
            R["o", u] = f

        def outp(u, i):
            g, b = units[u]
            w = g % 2
            z = yb
            ts = slice(128 * i, 128 * i + 128)
            terms = []
            for h in range(2):
                terms += [(OH[:, h, ts], woh[:, w, h, :]), (OH[:, h, ts], wol[:, w, h, :]), (OL[:, h, ts], woh[:, w, h, :])]
            m = self.mm(z[:], terms, R["o", u], split[g][1], *z.free, mark=True)
            x = self.X[:, 2 * b + i, :]
            f = self.tt(x, x, z[:], ALU.add, m, self.xtok[2 * b + i])
            z.free = [f]
            self.xtok[2 * b + i] = f
            R["Y", u] = m
            done[("y", g)] = m
            if g == 7:
                self.stat(2 * b + i)
                if not l0:
                    if b + i == 0:
                        self.early = self.ln_steps(each=True)
                    else:
                        next(self.early)

        n = len(units)
        fetch(0)
        for t in range(4):
            next(lns, None)
        part(0)
        proj(0)
        if not l0:
            late(0)
        scores(0)
        norm(0)
        for u in range(n):
            for step in "QT0S1PNE" if l0 else "Q0TL1SPNE":
                if step == "Q" and u + 1 < n:
                    proj(u + 1)
                if step == "T":
                    turn_p(u)
                if step == "L" and u + 1 < n and not l0:
                    late(u + 1)
                if step == "S" and u + 1 < n:
                    scores(u + 1)
                if step == "0":
                    if u + 2 < NB:
                        next(lns, None)
                        next(lns, None)
                    if u >= 1:
                        outp(u - 1, 0)
                if step == "1" and u >= 1:
                    outp(u - 1, 1)
                if step == "P":
                    pv_mm(u)
                if step == "E":
                    pv_out(u)
                if step == "N" and u + 1 < n:
                    norm(u + 1)
        outp(n - 1, 0)
        outp(n - 1, 1)
    def bcast(self, name, t, src):
        n = int(np.prod(src.shape))
        return self.load(name, t, src.rearrange("(a n) -> a n", a=1).to_broadcast([128, n]))

    def split_w(self, raw, hi, lo, *waits):
        f = self.copy_a(hi, raw, *waits)
        return self.tt(lo, raw, hi.bitcast(F32), ALU.subtract, f)

    def size(self, raw, i):
        j = i % 2
        names = ["L1_ffn_W_up", "L1_ffn_W_gate", "L1_ffn_W_down"]
        if i == 0:
            self.raw_free = [None, None]
        m = self.load(f"raw{j}", raw[:, j, :, :], self.ins[names[i // 4]][i % 4], self.raw_free[j])
        r = raw[:, j, :, :].rearrange("p c n -> p (c n)")
        self.sizes = self.raw_free[j] = self.act(r, r, ACT.Abs, m, accum_out=self.s12[:, i:i + 1])

    def ternary_ffn(self):
        V, A, G = self.V, self.A, self.G
        self.fence()
        raw = self.sb("raw", [128, 2, 4, 512], F32)
        TT = [self.sb(n, [128, 2, 4, 512], F32R) for n in ("Tu", "Tg", "Td")]
        neg = self.sb("neg", [128, 512], F32)
        HH, HL = (self.sb(n, [128, 2, 4, 256], F32R) for n in ("HH", "HL"))
        sl = self.sb("sl", [128, 512], F32)
        hf = self.sb("hf", [128, 2, 512], F32)
        s3 = self.sb("s3", [128, 6, 3], F32)
        names = ["L1_ffn_W_up", "L1_ffn_W_gate", "L1_ffn_W_down"]
        free = [None, None]
        if self.sizes is None:
            for i in range(12):
                self.size(raw, i)
            free = list(self.raw_free)
        s = self.red(s3[:, 0, :], self.s12[:].rearrange("p (w g) -> p w g", w=3), ALU.add, self.sizes)
        z = self.banks[2]
        m = self.mm(z[:, 0:3], [(self.ones[:], s3[:, 0, :])], s, mark=True)
        scale, half, nhalf, sgd = s3[:, 1, :], s3[:, 2, :], s3[:, 3, :], s3[:, 4, 0:1]
        s = self.ts(scale, z[:, 0:3], 2.0 ** -20, 1e-8, ALU.mult, ALU.add, m)
        z.free = [s]
        a = self.ts(half, scale, 0.5, None, ALU.mult, None, s)
        b = self.ts(nhalf, scale, -0.5, None, ALU.mult, None, s)
        scaled = self.tt(sgd, scale[:, 1:2], scale[:, 2:3], ALU.mult, s)
        self.ln_all()
        tern, done, R = {}, {}, {"raw": 0, "neg": None}

        def make(g, which=range(3)):
            marks = tern.setdefault(g, [])
            for w in which:
                j = R["raw"] % 2
                R["raw"] += 1
                m = self.load(f"raw{j}", raw[:, j, :, :], self.ins[names[w]][g], free[j])
                for c in range(4):
                    r = raw[:, j, c, :]
                    a = self.ts(neg[:], r, nhalf[:, w:w + 1], None, ALU.is_lt, None, m, R["neg"], scaled)
                    b = self.stt(TT[w][:, g % 2, c, :], r, half[:, w:w + 1], neg[:], ALU.is_gt, ALU.subtract, a,
                                 done.get((w, g - 2)))
                    R["neg"] = b
                free[j] = b
                marks.append(b)

        units = [(g, b) for g in range(4) for b in range(NB)]
        ub, gb, yb = self.banks[2:4], self.banks[4:6], self.banks[6:8]

        def up(u):
            g, b = units[u]
            w, j = g % 2, u % 2
            tok = slice(256 * b, 256 * b + 256)
            for cp in range(2):
                for W, z in ((0, ub[cp]), (1, gb[cp])):
                    for i in range(2):
                        hid = slice(256 * cp + 128 * i, 256 * cp + 128 * i + 128)
                        terms = []
                        for c in range(4):
                            t = TT[W][:, w, c, hid]
                            terms += [(t, self.XH[:, c, tok]), (t, self.XL[:, c, tok])]
                        m = self.mm(z[:, 256 * i:256 * i + 256], terms, tern[g][W], self.xnt[2 * b], self.xnt[2 * b + 1],
                                    *z.free, mark=i == 1)
                    done[(W, g)] = m
                    if W == 0:
                        f = self.act(sl[:], z[:], ACT.Silu, m, R.get("sl"), scale=scale[:, 0:1])
                        z.free = [f]
                p = cp
                f = self.stt(hf[:, p, :], gb[cp][:], sgd, sl[:], ALU.mult, ALU.mult, m, f, R.get(("hf", p)))
                gb[cp].free = [f]
                R["sl"] = f
                hh = HH[:, j, 2 * cp:2 * cp + 2, :].rearrange("p c n -> p (c n)")
                hl = HL[:, j, 2 * cp:2 * cp + 2, :].rearrange("p c n -> p (c n)")
                f = self.copy_a(hh, hf[:, p, :], f, R.get(("down", u - 2)))
                f = self.tt(hl, hf[:, p, :], hh.bitcast(F32), ALU.subtract, f, R.get(("down", u - 2)), eng=G)
                R["hf", p] = f
            R["h", u] = f

        def down(u):
            g, b = units[u]
            w, j = g % 2, u % 2
            for i in range(2):
                z = yb[i]
                ts = slice(128 * i, 128 * i + 128)
                terms = []
                for c in range(4):
                    t = TT[2][:, w, c, :]
                    terms += [(HH[:, j, c, ts], t), (HL[:, j, c, ts], t)]
                m = self.mm(z[:], terms, R["h", u], tern[g][2], *z.free, mark=True)
                x = self.X[:, 2 * b + i, :]
                f = self.tt(x, x, z[:], ALU.add, m, self.xtok[2 * b + i])
                z.free = [f]
                self.xtok[2 * b + i] = f
                if g == 3:
                    self.stat(2 * b + i)
                    if b + i == 0:
                        self.early = self.ln_steps(plain=self.XF, each=True)
                    else:
                        next(self.early)
            R["down", u] = m
            done[(2, g)] = m

        make(0)
        up(0)
        for u in range(len(units)):
            if u % 8 in (2, 3, 4) and u // 8 < 3:
                make(u // 8 + 1, [u % 8 - 2])
            if u + 1 < len(units):
                up(u + 1)
            down(u)

    def add_factor(self, raw, acc, r):
        if r == 0:
            self.facts = self.load("raw2", acc[:], self.ins["L2_ffn_factors"][0])
            return
        j = r % 2
        if self.coming is not None:
            k, m = self.coming
            self.facts = self.raw_free[k] = self.tt(acc[:], acc[:], raw[:, k, :, :], ALU.add, m, self.facts)
            self.coming = None
        if r < 8:
            self.coming = j, self.load(f"raw{j}", raw[:, j, :, :], self.ins["L2_ffn_factors"][r], self.raw_free[j])
        else:
            self.factors = self.load("fsum", self.FS, acc[:], self.facts)

    def mix(self):
        V = self.V
        self.fence()
        acc = self.sb("acc", [128, 4, 512], F32)
        fh, fl = (self.sb(n, [128, 4, 512], F32R) for n in ("fh", "fl"))
        bias = self.sb("bias", [128, 512], F32)
        tmp = self.sb("tmp", [128, 2, 512], F32)
        mb = self.bcast("bias", bias[:], self.ins["L2_ffn_bias"])
        if self.factors is None:
            raw = self.sb("raw", [128, 2, 4, 512], F32)
            self.raw_free = [None, None]
            for r in range(9):
                self.add_factor(raw, acc, r)
        f = self.load("raw2", acc[:], self.FS, self.factors)
        w = self.split_w(acc[:], fh[:], fl[:], f)
        self.ln_all()
        done = {}
        for t in range(NT):
            z = self.banks[2 + t % 4]
            tok = slice(128 * t, 128 * t + 128)
            terms = []
            for c in range(4):
                xh, xl = self.XH[:, c, tok], self.XL[:, c, tok]
                terms += [(xh, fh[:, c, :]), (xh, fl[:, c, :]), (xl, fh[:, c, :])]
            m = self.mm(z[:], terms, w, self.xnt[t], *z.free, mark=True)
            a = self.stt(tmp[:, t % 2, :], z[:], 8.0 ** -0.5, bias[:], ALU.mult, ALU.add, m, mb, done.get(t - 2))
            z.free = [a]
            x = self.X[:, t, :]
            done[t] = self.xtok[t] = self.tt(x, x, tmp[:, t % 2, :], ALU.add, a, self.xtok[t], eng=self.G)
            if t >= 2:
                self.stat(t - 2)
        self.stat(NT - 2)
        self.stat(NT - 1)

    def choice(self):
        V, A = self.V, self.A
        self.fence()
        raw = self.sb("raw", [128, 4, 512], F32)
        wh, wl = (self.sb(n, [128, 4, 512], F32R) for n in ("wh", "wl"))
        rr = self.sb("rr", [128, 4, 16], F32)
        rh, rl = (self.sb(n, [128, 4, 16], F32R) for n in ("rh", "rl"))
        rb = self.sb("rb", [128, 16], F32)
        eb = self.sb("eb", [128, 512], F32)
        Y = self.sb("Y", [128, NT, 512], F32)
        LG = self.sb("LG", [128, NT, 16], F32)
        sm = self.sb("sm", [128, 3, NT], F32)
        ST = self.sb("ST", [16, T], F32)
        WK = self.sb("WK", [16, T], F32)
        m8 = self.sb("m8", [16, 2, 8], F32)
        cc = self.sb("cc", [128, NT], F32)
        m1 = self.load("raw0", raw[:], self.ins["L3_ffn_expert_w"])
        m2 = self.load("raw1", rr[:], self.ins["L3_ffn_router_w"])
        m3 = self.bcast("rb", rb[:], self.ins["L3_ffn_router_b"])
        m4 = self.bcast("eb", eb[:], self.ins["L3_ffn_expert_b"])
        r = self.split_w(rr[:], rh[:], rl[:], m2)
        w = self.split_w(raw[:], wh[:], wl[:], m1)
        lg, m = self.route(16, rh, rl, WK, r)
        f = self.tt(LG[:], lg, rb[:].unsqueeze(1).to_broadcast([128, NT, 16]), ALU.add, m, m3)
        self.banks[2].free = [f]
        s = self.red(sm[:, 0, :], LG[:], ALU.max, f)
        s = self.tt(LG[:], LG[:], sm[:, 0, :].unsqueeze(2).to_broadcast([128, NT, 16]), ALU.subtract, s)
        s = self.act(LG[:], LG[:], ACT.Exp, s)
        a = self.red(sm[:, 1, :], LG[:], ALU.add, s)
        a = V.do(lambda e: e.reciprocal(sm[:, 2, :], sm[:, 1, :]), a)
        s = self.tt(LG[:], LG[:], sm[:, 2, :].unsqueeze(2).to_broadcast([128, NT, 16]), ALU.mult, a)
        for k in range(4):
            z = self.banks[2 + k % 2]
            for i in range(4):
                m = self.transpose(z[0:16, 128 * i:128 * i + 128], LG[:, 4 * k + i, :], s, *z.free, mark=i == 3)
            f = self.copy_a(ST[:, 512 * k:512 * k + 512], z[0:16, :], m)
            z.free = [f]
        for t in range(NT):
            z = self.banks[4 + t % 2]
            tok = slice(128 * t, 128 * t + 128)
            terms = []
            for c in range(4):
                xh, xl = self.XH[:, c, tok], self.XL[:, c, tok]
                terms += [(xh, wh[:, c, :]), (xh, wl[:, c, :]), (xl, wh[:, c, :])]
            m = self.mm(z[:], terms, w, *z.free, mark=True)
            y = self.copy_a(Y[:, t, :], z[:], m)
            z.free = [y]
            y = self.tt(Y[:, t, :], Y[:, t, :], eb[:], ALU.add, y, m4, eng=self.G)
        cur = ST
        o = None
        for i in range(16):
            a = V.do(lambda e, i=i, cur=cur: e.max(m8[:, i % 2, :], cur[:]), f)
            f = V.do(lambda e, i=i, cur=cur: e.match_replace(WK[:], m8[:, i % 2, :], cur[:], -1.0), a)
            cur = WK
        f = self.stt(ST[:], WK[:], 0.0, ST[:], ALU.is_lt, ALU.mult, f)
        z = self.banks[2]
        for t in range(NT):
            m = self.mm(z[:, t:t + 1], [(ST[:, 128 * t:128 * t + 128], self.ones[0:16, 0:1])], f, *z.free, mark=t == NT - 1)
        f = self.copy_v(cc[:], z[:, 0:NT], m)
        z.free = [f]
        for t in range(NT):
            x = self.X[:, t, :]
            self.xtok[t] = self.stt(x, Y[:, t, :], cc[:, t:t + 1], x, ALU.mult, ALU.add, f, y, self.xtok[t])

    def attend_narrow(self, L):
        A, V, G, PE = self.A, self.V, self.G, self.PE
        l1 = L == 1
        H, HD = (16, 32) if l1 else (32, 16)
        SC = float(HD) ** -0.5
        NP_ = H // 2
        self.fence()
        XF = self.XF
        xl = [self.xl_at]

        def side(name, shape, dt):
            t = self.at(name, shape, dt, xl[0])
            xl[0] += -(-int(np.prod(shape[1:])) * mybir.dt.size(dt) // 32) * 32
            assert xl[0] <= self.xl_at + 32768
            return t

        pre = f"L{L}_xattn_"
        wq = self.sb("nwq", [128, 4, 512], F32)
        wkv = self.sb("nwkv", [128, 2, 1024], F32)
        wo = self.sb("nwo", [128, 4, 512], F32)
        kT = [self.sb("kT0", [128, 16, 256], F32R), None]
        over = xl[0]
        kT[1] = side("kT1", [128, 16, 256], F32R)
        bo = side("nbo", [128, 512], F32)
        qT = self.sb("nqT", [128, 2, 16, 128], F32R)
        stk = self.sb("stk", [128, 16, 128], F32R)
        VV = self.sb("nV", [128, 2, 2, 32 * H], F32)
        PT = self.sb("nPT", [128, 2, 4, 128], F32)
        OT = self.sb("nOT", [128, 4, 128], F32)
        cbk = [self.sb("ncb0", [128, 512], F32), side("ncb1", [128, 512], F32)]
        st4 = self.sb("nst", [128, 4, 16], F32)
        mx, nb, sm, rc = (self.sb(n, [128, 5, 4], F32) for n in ("nmx", "nnb", "nsm", "nrc"))
        depth, np_ = 4, 4
        more = [(self.sb if l1 else side)(f"nP{i}", [128, 2, 256], F32) for i in range(2, np_)]
        mq = self.load("raw0", wq[:], self.ins[pre + "Wq"])
        mk = self.load("raw1", wkv[:], self.ins[pre + "Wkv"])
        mo = self.load("wo", wo[:], self.ins[pre + ("Wo" if l1 else "Wout")])
        mbo = self.bcast("bias", bo[:], self.ins[pre + ("bo" if l1 else "bout")])
        R = {}
        if l1:
            bkv = self.sb("nbkv", [128, 1024], F32)
            bq = side("nbq", [128, 512], F32)
            kdT = side("kdT", [128, 16, 128], F32R)
            Vd = side("Vd", [128, 512], F32)
            cd = self.at("ncd", [128, 2, 128], F32, over + 12288)
            wd = self.at("nwd", [128, 2, 1024], F32, over)
            bd = self.at("nbd", [128, 1024], F32, over + 8192)
            vec = {n: self.sb("v" + n, [128, 32], F32) for n in ("qn_w", "qn_b", "kn_w", "kn_b", "kn_dca_w", "kn_dca_b")}
            md = self.load("wd", wd[:], self.ins[pre + "Wkv_dca"])
            mc = self.load("cd", cd[:], self.ins["ctx_dcaT"])
            mb = self.bcast("b1", bd[:], self.ins[pre + "bkv_dca"])
            mb = self.bcast("b1", bkv[:, 0:512], self.ins[pre + "bk"])
            mb = self.bcast("b1", bkv[:, 512:1024], self.ins[pre + "bv"])
            mb = self.bcast("b1", bq[:], self.ins[pre + "bq"])
            for n, t in vec.items():
                mb = self.bcast("b1", t[:], self.ins[pre + n])
        else:
            pos = side("pos", [128, NT, 2], F32)
            ang = self.at("ang", [128, NT, 2, 4], F32, over)
            kk = self.at("kk", [128, NT * 8], F32, over + 512)
            rr = self.at("rr", [128, NT * 8], F32, over + 1024)
            cs = [side(n, [128, NT, 8], F32) for n in ("cosT", "sinT")]
            m1b = side("m1b", [128, 512], F32)
            m2b = side("m2b", [128, 512], F32)
            m = self.load("b1", pos[:], self.ins["fside_BxSx2_0"].rearrange("b (t p) c -> p (b t) c", p=128))
            freqs = np.float32(10000.0) ** (-np.arange(4, dtype=np.float32) / np.float32(4))
            for j in range(4):
                a = self.ts(ang[:, :, :, j], pos[:], float(freqs[j]), None, ALU.mult, None, m)
            ang = ang[:].rearrange("p t c j -> p (t c j)")
            c1 = np.float32(6.28125)
            c2 = np.float32(2 * np.pi - 6.28125)
            c3 = np.float32(2 * np.pi - 6.28125 - float(c2))
            for w, (quarter, shift) in enumerate(((0.25, np.pi / 2), (0.0, 0.0))):
                a = self.ts(kk[:], ang, 1 / (2 * np.pi), quarter, ALU.mult, ALU.add, a)
                a = self.ts(kk[:], kk[:], 12582912.0, 12582912.0, ALU.add, ALU.subtract, a)
                a = self.stt(rr[:], kk[:], -float(c1), ang, ALU.mult, ALU.add, a)
                a = self.stt(rr[:], kk[:], -float(c2), rr[:], ALU.mult, ALU.add, a)
                a = self.stt(rr[:], kk[:], -float(c3), rr[:], ALU.mult, ALU.add, a)
                a = self.ts(rr[:], rr[:], float(shift), 3.1415925, ALU.add, ALU.min, a)
                a = self.ts(rr[:], rr[:], -3.1415925, None, ALU.max, None, a)
                a = self.act(cs[w][:].rearrange("p t c -> p (t c)"), rr[:], ACT.Sin, a)
            mb = a
        cen = None
        if l1:
            def center(v, n, *waits):
                m = avg[:, 0:n]
                a = self.red(m, v, ALU.add, *waits)
                a = self.ts(m, m, 1.0 / 32, None, ALU.mult, None, a)
                return self.tt(v, v, m.unsqueeze(2).to_broadcast([128, n, 32]), ALU.subtract, a)

            avg = st4[:].rearrange("p a h -> p (a h)")
            cols = lambda v: v.rearrange("p (h d) -> p h d", d=32)
            cen = center(wq[:].rearrange("p c (h d) -> p (c h) d", d=32), 64, mq)
            cen = center(wkv[:].rearrange("p c (h e d) -> p (c h) e d", e=2, d=32)[:, :, 0, :], 32, mk, cen)
            for c in range(2):
                cen = center(cols(wd[:, c, 0:512]), 16, md, cen)
            cen = center(cols(bd[:, 0:512]), 16, mb, cen)
            cen = center(cols(bq[:]), 16, cen)
            cen = center(bkv[:].rearrange("p (h e d) -> p h e d", e=2, d=32)[:, :, 0, :], 16, cen)
        xn_free = self.ln_all(plain=XF)
        Pb = [self.at(f"nP{i}", [128, 2, 256], F32, self.xn_at + 2048 * i) for i in range(2)] + more

        pbank, tbank = self.banks[0], self.banks[1]

        def old(*key):
            return R[key] if key[1] >= 0 else None

        wide = lambda v: v[:].rearrange("p (h d) -> p h d", d=HD)

        def square(src, z, f, k):
            f = self.act(z[:], src, ACT.Square, f)
            yield
            f = self.red(st4[:, k, :], z[:].rearrange("p (h d) -> p h d", h=16), ALU.add, f)
            z.free = [f]
            f = self.ts(st4[:, k, :], st4[:, k, :], 1.0 / 32, 1e-6, ALU.mult, ALU.add, f)
            f = self.rsqrt(st4[:, k + 1, :], st4[:, k, :], f)
            for _ in range(3):
                yield
            return f

        def scale(c3, w, b, f, k):
            g = 16 // c3.shape[1] if len(c3.shape) == 4 else 0
            rs = st4[:, k + 1, :]
            if g:
                rs = rs.rearrange("p (c h) -> p c h", h=g).unsqueeze(3).to_broadcast(list(c3.shape))
                row = lambda v: v[:].unsqueeze(1).unsqueeze(1).to_broadcast(list(c3.shape))
            else:
                rs = rs.unsqueeze(2).to_broadcast(list(c3.shape))
                row = lambda v: v[:].unsqueeze(1).to_broadcast(list(c3.shape))
            f = self.tt(c3, c3, rs, ALU.mult, f)
            f = self.tt(c3, c3, row(w), ALU.mult, f, mb, eng=G)
            return self.tt(c3, c3, row(b), ALU.add, f, eng=G)

        def rope(t, z, m, oo, *free):
            zz = z[:].rearrange("p (h c d) -> p h c d", h=32, d=2)
            m1, m2 = (x[:].rearrange("p (h c d) -> p h c d", h=32, d=2) for x in (m1b, m2b))
            f = None
            for d in range(2):
                tab = lambda w: cs[w][:, t, :].unsqueeze(1).to_broadcast([128, 32, 8])
                self.tt(m1[:, :, :, d], zz[:, :, :, d], tab(0), ALU.mult, m, mb, R.get("rope"))
                f = self.tt(m2[:, :, :, d], zz[:, :, :, d], tab(1), ALU.mult)
            z.free = [f]
            yield
            g = self.tt(oo(0), halves(m1, 0), halves(m2, 1), ALU.subtract, f, *free, eng=G)
            g = self.tt(oo(1), halves(m2, 0), halves(m1, 1), ALU.add, f, eng=G)
            R["rope"] = g
            yield
            return g

        def halves(m, d):
            return m[:, :, :, d].rearrange("p (c h) e -> p c h e", c=4)

        def project(z, w, x, *waits):
            n = len(x)
            for c in range(n):
                m = self.mm(z[:], [(x[c], w(c))], *waits, *z.free, mark=c == n - 1, start=c == 0, stop=c == n - 1)
                if c % 2:
                    yield
            return m

        def norm_q(t, z=pbank):
            tok = slice(128 * t, 128 * t + 128)
            m = yield from project(z, lambda c: wq[:, c, :], [XF[:, c, tok] for c in range(4)], mq, cen, self.xnt[t])
            q = XF[:, :, tok]
            if l1:
                f = self.tt(q, z[:].rearrange("p (c n) -> p c n", c=4), bq[:].rearrange("p (c n) -> p c n", c=4), ALU.add, m, mb)
                yield
                f = yield from square(q, z, f, 0)
                yield
                f = scale(q.rearrange("p c (h d) -> p c h d", d=32), vec["qn_w"], vec["qn_b"], f, 0)
            else:
                qq = q.rearrange("p c (h e d) -> p c h e d", e=8, d=2)
                f = yield from rope(t, z, m, lambda d: qq[:, :, :, :, d])
            R["qn", t] = f
            yield

        def norm_k(t, z=pbank):
            tok = slice(128 * t, 128 * t + 128)
            cb = cbk[t % 2]
            free = R.get(("kd", t - 2), [])
            if l1:
                w = lambda c: wkv[:, c, :].rearrange("p (h e d) -> p h e d", e=2, d=32)[:, :, 0, :]
            else:
                w = lambda c: wkv[:, c, 0:512]
            m = yield from project(z, w, [self.CTX[:, c, tok] for c in range(2)], mk, cen, self.ctxtok)
            if l1:
                f = self.tt(wide(cb), wide(z.t), bkv[:].rearrange("p (h e d) -> p h e d", e=2, d=32)[:, :, 0, :], ALU.add, m, mb, *free)
                yield
                f = yield from square(cb[:], z, f, 2)
                yield
                f = scale(wide(cb), vec["kn_w"], vec["kn_b"], f, 2)
            else:
                kk_ = cb[:].rearrange("p (c h e d) -> p c h e d", c=4, e=8, d=2)
                f = yield from rope(t, z, m, lambda d: kk_[:, :, :, :, d], *free)
            R["kn", t] = f
            yield

        def values(t, z=pbank):
            b, i = t // 2, t % 2
            j = b % 2
            tok = slice(128 * t, 128 * t + 128)
            if l1:
                w = lambda c: wkv[:, c, :].rearrange("p (h e d) -> p h e d", e=2, d=32)[:, :, 1, :]
            else:
                w = lambda c: wkv[:, c, 512:1024]
            m = yield from project(z, w, [self.CTX[:, c, tok] for c in range(2)], mk, self.ctxtok)
            if l1:
                f = self.tt(wide(VV[:, j, i, :]), wide(z.t), bkv[:].rearrange("p (h e d) -> p h e d", e=2, d=32)[:, :, 1, :],
                            ALU.add, m, mb, old("O", b - 2))
                if i == 1:
                    R["v", b, 1] = self.load(f"vd{j}", VV[112:128, j, 1, :], Vd[16 * b:16 * b + 16, :], f, R["vd"])
                else:
                    R["v", b, 0] = f
            else:
                for e in range(2):
                    vv = VV[:, j, i, :].rearrange("p (h e d) -> p h e d", e=2, d=32)[:, :, e, 16 * e:16 * e + 16]
                    f = self.copy_a(vv, z[:].rearrange("p (h e d) -> p h e d", e=2, d=16)[:, :, e, :], m, old("O", b - 2), cleared)
                R["v", b, i] = f
            z.free = [f]
            yield

        def stack(f, src, queries, dst, n, *free):
            if len(src.shape) == 4:
                v = stk[:].rearrange("p a b -> p (a b)").rearrange("p (c h s d) -> p c h s d", c=4, s=128 // HD if l1 else 4, d=HD)
                part = lambda s: v[:, :, :, s, :]
            else:
                v = stk[:].rearrange("p a b -> p (a b)").rearrange("p (h s d) -> p h s d", h=H, d=HD)
                part = lambda s: v[:, :, s, :]
            hi = part if queries else (lambda s: part(2 * s))
            lo = (lambda s: part(2 + s)) if queries else (lambda s: part(2 * s + 1))
            for s in range(2):
                a = self.copy_a(hi(s), src, f, R.get("stk"))
            yield
            b0 = self.tt(lo(0), src, hi(0).bitcast(F32), ALU.subtract, a)
            b1 = self.tt(lo(1), src, hi(0).bitcast(F32), ALU.subtract, a, eng=None if l1 else G)
            for _ in range(1 if l1 else 2):
                yield
            marks = []
            z = tbank
            for k in range(4):
                for i in range(4):
                    m = self.transpose(z[:, 128 * i:128 * i + 128], stk[:, 4 * k + i, :].bitcast(F32), b0, b1, *z.free, mark=i == 3)
                src4 = z[:].rearrange("p (h n) -> p h n", h=4)[:, :, 0:n]
                g = (self.copy_a if k % 2 else self.copy_v)(dst(k), src4, m, *free)
                z.free = [g]
                marks.append(g)
                yield
            R["stk"] = m
            return marks, [b0, b1]

        def drain(g):
            for _ in g:
                pass

        def stack_q(t):
            j = t % 2
            q = XF[:, :, 128 * t:128 * t + 128].rearrange("p c (h d) -> p c h d", d=HD)
            R["q", t], _ = yield from stack(R["qn", t], q, True, lambda k: qT[:, j, 4 * k:4 * k + 4, :], 128, old("Sq", t - 2))

        def stack_k(t):
            b, i = t // 2, t % 2
            n = 112 if l1 and i else 128
            dst = kT[b % 2]
            marks, R["kd", t] = yield from stack(
                R["kn", t], wide(cbk[t % 2]), False, lambda k: dst[:, 4 * k:4 * k + 4, 128 * i:128 * i + n], n,
                old("S", b - 2), *R.get("over", []))
            if l1 and i:
                marks.append(self.copy_a(dst[:, :, 240:256], kdT[:, :, 16 * b:16 * b + 16].bitcast(F32), *R["kdca"]))
            R["k", b] = R.get(("k", b), []) + marks

        def dca():
            z, cb = pbank, cbk[0]
            m = yield from project(z, lambda c: wd[:, c, 512:1024], [cd[:, c, :] for c in range(2)], md, mc)
            z.free = [self.tt(Vd[:], z[:], bd[:, 512:1024], ALU.add, m, mb)]
            R["vd"] = z.free[0]
            m = yield from project(z, lambda c: wd[:, c, 0:512], [cd[:, c, :] for c in range(2)], cen)
            f = self.tt(cb[:], z[:], bd[:, 0:512], ALU.add, m)
            g = f
            f = yield from square(cb[:], z, f, 2)
            f = scale(wide(cb), vec["kn_dca_w"], vec["kn_dca_b"], f, 2)
            R["kdca"], R["kd", -2] = yield from stack(f, wide(cb), False, lambda k: kdT[:, 4 * k:4 * k + 4, :], 128)
            R["over"] = [g]

        if not l1:
            cleared = G.do(lambda e: e.memset(VV[:], 0.0))

        steps = [(t, p) for t in range(NT) for p in range(NP_)]
        n = len(steps)
        heads = lambda p: (2 * p, 2 * p + 1) if l1 else (4 * (p // 2) + p % 2, 4 * (p // 2) + p % 2 + 2)
        sbk, tbk, obk, ybk = self.banks[2:4], self.banks[4:6], self.banks[6], self.banks[7]
        parts = ((0, 240), (240, 256)) if l1 else ((0, 256),)
        w = 2 * len(parts)

        def scores(s):
            t, p = steps[s]
            b, j = t // 2, s % 3
            z = sbk[s % 2]
            for i, h in enumerate(heads(p)):
                if l1:
                    l, r = qT[:, t % 2, h, :], kT[b % 2][:, h, :]
                else:
                    rows = slice(64 * (h % 2), 64 * (h % 2) + 64)
                    l, r = qT[rows, t % 2, h // 2, :], kT[b % 2][rows, h // 2, :]
                m = self.mm(z[:, 256 * i:256 * i + 256], [(l, r)], *R["q", t], *R["k", b], *z.free, mark=i == 1)
            R["s", s] = m
            if p == NP_ - 1:
                R["Sq", t] = m
                if t % 2:
                    R["S", b] = m

        def soften(s):
            t, p = steps[s]
            j = s % np_
            z, P, m = sbk[s % 2], Pb[j], R["s", s]
            zz = z[:].rearrange("p (h n) -> p h n", h=2)
            for k, (a, e) in enumerate(parts):
                f = self.red(mx[:, j, 2 * k:2 * k + 2], zz[:, :, a:e], ALU.max, m, R.get(("nb", s - np_)), negate=True)
            f = self.ts(nb[:, j, 0:w], mx[:, j, 0:w], SC, None, ALU.mult, None, f, R.get(("E", s - np_)))
            R["nb", s] = f
            for k, (a, e) in enumerate(parts):
                for i in range(2):
                    g = self.act(P[:, i, a:e], zz[:, i, a:e], ACT.Exp, f, R.get(("T", s - np_)), R.get(("N", s - np_)), xn_free,
                                 bias=nb[:, j, 2 * k + i:2 * k + i + 1], scale=SC, accum_out=sm[:, j, 2 * k + i:2 * k + i + 1])
            z.free = [g]
            R["E", s] = g

        def norm(s):
            j = s % np_
            r = V.do(lambda e: e.reciprocal(rc[:, j, 0:w], sm[:, j, 0:w]), R["E", s], R.get(("N", s - np_)))
            for k, (a, e) in enumerate(parts):
                g = self.tt(Pb[j][:, :, a:e], Pb[j][:, :, a:e], rc[:, j, 2 * k:2 * k + 2].unsqueeze(2).to_broadcast([128, 2, e - a]),
                            ALU.mult, r, eng=G)
            R["N", s] = g

        def turn_p(s):
            j = s % 2
            z, P = tbk[j], Pb[s % np_]
            for kt in range(2):
                for i in range(2):
                    k = 2 * kt + i
                    m = self.transpose(z[:, 128 * k:128 * k + 128], P[:, i, 128 * kt:128 * kt + 128], R["N", s], *z.free,
                                       mark=k == 3)
            R["T", s] = m
            f = (self.copy_a if l1 or s % 3 == 0 else self.copy_v)(PT[:, j, :, :].rearrange("p a n -> p (a n)"), z[:], m,
                                                                   R.get(("pv", s - 2)))
            z.free = [f]
            R["pt", s] = f

        def pv(s):
            t, p = steps[s]
            b, j = t // 2, s % 2
            z = obk
            for i, h in enumerate(heads(p)):
                r = 32 * (h if l1 else h // 2)
                first, last = (True, True) if l1 else (h % 2 == 0, h % 2 == 1)
                m = self.mm(z[r % 128:r % 128 + 32, r // 128 * 128:r // 128 * 128 + 128],
                            [(VV[:, b % 2, kt, 32 * h:32 * h + 32], PT[:, j, 2 * kt + i, :]) for kt in range(2)],
                            R["pt", s], R["v", b, 0], R["v", b, 1], *z.free, mark=i == 1, start=first, stop=last, skip=not l1)
            R["pv", s] = m
            if p == NP_ - 1:
                if t % 2:
                    R["O", b] = m
                f = self.copy_a(OT[:].rearrange("p c n -> p (c n)"), z[:], m, R.get("y"))
                z.free = [f]
                R["oT"] = f

        def outp(t, c):
            z = ybk
            m = self.mm(z[:], [(OT[:, c, :], wo[:, c, :])], R["oT"], mo, *z.free, mark=c == 3, start=c == 0, stop=c == 3)
            R["y"] = R["y", t] = m

        def add(t):
            z = ybk
            x = self.X[:, t, :]
            f = self.tt(x, x, z[:], ALU.add, R["y", t], self.xtok[t])
            z.free = [f]
            self.xtok[t] = self.tt(x, x, bo[:], ALU.add, f, mbo, eng=G)

        def ahead_a(t):
            if t + 2 < NT:
                yield from norm_q(t + 2)
            if t + 3 < NT:
                yield from norm_k(t + 3)
            if t + 2 < NT:
                yield from values(t + 2)

        def ahead_b(t):
            if t + 1 < NT:
                yield from stack_q(t + 1)
            if t + 2 < NT:
                yield from stack_k(t + 2)

        free = self.banks[2:6]
        for group in ([norm_q(0, free[0])] + ([dca()] if l1 else []),
                      [stack_q(0), norm_k(0)],
                      [stack_k(0), norm_k(1), norm_q(1, free[1])],
                      [stack_k(1), norm_k(2), values(0, free[2]), values(1, free[3])]):
            while group:
                for g in list(group):
                    if next(g, group) is group:
                        group.remove(g)
        preps = []
        pieces = (21, 13) if l1 else (11, 15)
        for s in range(-depth, n + 1):
            u = s + depth
            if u < n and u % NP_ == 0:
                for g in preps:
                    drain(g)
                preps = [ahead_a(u // NP_), ahead_b(u // NP_)]
            q = u % NP_
            due = [c * (q + 1) // NP_ - c * q // NP_ for c in pieces]

            def advance(i):
                if preps and due[i] > 0:
                    due[i] -= 1
                    next(preps[i], None)

            for step in "NSPTBAFOABA" if l1 else "TNAASPBABFO":
                if step == "T" and 0 <= s < n:
                    turn_p(s)
                if step == "B":
                    advance(1)
                if step == "A":
                    advance(0)
                if step == "S" and u < n:
                    scores(u)
                if step == "F" and u < n:
                    soften(u)
                if step == "N" and 0 <= s + 2 < n:
                    norm(s + 2)
                if step == "P" and s >= 1:
                    pv(s - 1)
                if step == "O" and s >= 1:
                    t, p = steps[s] if s < n else (NT, 0)
                    if t >= 1 and 1 <= p <= 4:
                        outp(t - 1, p - 1)
                    if t >= 1 and p == 5:
                        add(t - 1)
                    if t >= 1 and p == 7:
                        self.stat(t - 1)
        for c in range(4):
            outp(NT - 1, c)
        add(NT - 1)
        self.stat(NT - 1)

    def attend_l1(self):
        self.attend_narrow(1)

    def attend_l2(self):
        self.attend_narrow(2)

    def experts(self):
        A, V, G, PE, SP = self.A, self.V, self.G, self.PE, self.SP
        while self.cleared < 4:
            self.clear()
        self.fence()
        base = self.top
        WB = self.at("WB", [128, 3 * 6144], F32, base)
        XN = self.at("XN", [128, NT, D], F32, base + 49152)
        self.top = base + 81920
        rl = self.sb("erl", [128, 4, 8], F32)
        rsc = self.sb("ersc", [128, 4], F32)
        rh, rlo = (self.sb(n, [128, 4, 8], F32R) for n in ("erh", "erlo"))
        esc = self.sb("eesc", [128, 8], F32)
        LG = self.sb("eLG", [128, NT, 8], F32)
        m8 = self.sb("em8", [128, NT, 8], F32)
        i8 = self.sb("ei8", [128, NT, 8], U32)
        oh = self.sb("eoh", [128, 2, NT, 8], F32)
        OA = self.sb("eOA", [128, NT, 8], F32)
        cu = self.sb("ecu", [128, 2, NT, 8], F32)
        pos = self.sb("epos", [128, NT, 8], F32)
        tm = self.sb("etm", [128, NT, 8], F32)
        i8f = self.sb("ei8f", [128, 8], F32)
        sm = self.sb("esm", [128, 12, NT], F32)
        POS = self.sb("ePOS", [128, 2, NT], I32)
        e8 = self.sb("ee8", [128, 6, 8], F32)
        n8 = self.sb("en8", [128, 8], I32)
        jio = self.sb("ejio", [1, 40], F32)
        ge = self.at("ege", [1, 40, 8], F32, self.xl_at + 30720)
        eb = self.sb("eeb", [1, 8, 40], F32)
        EI = self.sb("eEI", [1, 4, 40], I32)
        up = [self.xh_at]

        def work(name, shape, dt):
            t = self.at(name, shape, dt, up[0])
            up[0] += -(-int(np.prod(shape[1:])) * mybir.dt.size(dt) // 32) * 32
            assert up[0] <= self.xl_at + 30720
            return t

        xs = work("exs", [128, 3, 512], F32)
        xsT = work("exsT", [128, 2, 4, 128], F32)
        gl = work("egl", [128, 512], F32)
        hh = work("ehh", [128, 2, 512], F32)
        hT = work("ehT", [128, 2, 4, 128], F32)
        os_ = work("eos", [128, 2, 512], F32)
        raw = work("eraw", [128, 2, 4, 512], F32)
        gt_at = up[0]
        gt = work("egt", [128, 4, 2, 512], F32)
        assert gt_at >= self.xl_at
        tri = work("etri", [128, 128], F32)

        m1 = self.load("raw0", rl[:], self.ins["L0_ffn_router_logits"])
        m2 = self.load("raw1", rsc[:], self.ins["L0_ffn_router_scale"])
        m3 = self.bcast("bias", esc[:], self.ins["L0_ffn_per_expert_scale"])
        f = self.tt(rl[:], rl[:], rsc[:].unsqueeze(2).to_broadcast([128, 4, 8]), ALU.mult, m1, m2)
        rw = self.split_w(rl[:], rh[:], rlo[:], f)
        a = G.do(lambda e: e.iota(i8f[:], [[1, 8]], base=0, channel_multiplier=0, allow_small_or_imprecise_dtypes=True))
        b = G.do(lambda e: e.iota(jio[:], [[1, 40]], base=0, channel_multiplier=0, allow_small_or_imprecise_dtypes=True))
        consts = b
        sq = [None, None]

        def square(t, d):
            sq[t % 2] = self.act(self.banks[6 + t % 2][:], XN[:, t, :], ACT.Square, d, sq[t % 2], accum_out=sm[:, 0, t:t + 1])

        lg, logits = self.route(8, rh, rlo, self.at("elgT", [8, T], F32, gt_at), rw, keep=XN, after=square)
        s = sq[(NT - 1) % 2]
        s = self.ts(sm[:, 1, :], sm[:, 0, :], 1.0 / 512, 1e-6, ALU.mult, ALU.add, s)
        s = self.rsqrt(sm[:, 2, :], sm[:, 1, :], s)
        s = self.ts(sm[:, 2, :], sm[:, 2, :], 512.0 ** -0.5, None, ALU.mult, None, s)
        f = self.tt(LG[:], lg, sm[:, 2, :].unsqueeze(2).to_broadcast([128, NT, 8]), ALU.mult, logits, s)
        self.banks[2].free = [f]
        for t in range(NT):
            f = V.do(lambda e, t=t: e.max(m8[:, t, :], LG[:, t, :]), f if t == 0 else None)
        for t in range(NT):
            f = V.do(lambda e, t=t: e.max_index(i8[:, t, :], m8[:, t, :], LG[:, t, :]), f if t == 0 else None)
        g = self.tt(sm[:, 3, :], m8[:, :, 1], m8[:, :, 0], ALU.subtract, f)
        g = self.act(sm[:, 4, :], sm[:, 3, :], ACT.Exp, g)
        g = self.ts(sm[:, 5, :], sm[:, 4, :], 1.0, None, ALU.add, None, g)
        g = V.do(lambda e: e.reciprocal(sm[:, 6, :], sm[:, 5, :]), g)
        wts = self.tt(sm[:, 7, :], sm[:, 4, :], sm[:, 6, :], ALU.mult, g)
        for k in range(2):
            f = self.copy_v(sm[:, 8 + k, :], i8[:, :, k], f)
        for k in range(2):
            g = self.tt(oh[:, k, :, :], i8f[:].unsqueeze(1).to_broadcast([128, NT, 8]),
                        sm[:, 8 + k, :].unsqueeze(2).to_broadcast([128, NT, 8]), ALU.is_equal, f, consts)
        g = self.tt(OA[:], oh[:, 0, :, :], oh[:, 1, :, :], ALU.add, g)
        c1 = G.do(lambda e: e.memset(tri[:], 1.0), logits)
        c1 = G.do(lambda e: e.affine_select(out=tri[:], in_=tri[:], compare_op=ALU.is_gt, fill=0.0, base=0,
                                            pattern=[[1, 128]], channel_multiplier=-1), c1)
        z = self.banks[2]
        oa = OA[:].rearrange("p t e -> p (t e)")
        self.mm(z[:, 0:128], [(tri[:], oa)], g, c1, *z.free)
        m = self.mm(z[:, 128:256], [(self.ones[:], oa)], mark=True)
        pre = z[:, 0:128].rearrange("p (t e) -> p t e", t=NT)
        tot = z[:, 128:256].rearrange("p (t e) -> p t e", t=NT)
        f = self.copy_v(cu[:, 0, :, :], tot, m)
        j = 0
        for k in (1, 2, 4, 8):
            self.copy_v(cu[:, 1 - j, 0:k, :], cu[:, j, 0:k, :], f)
            f = self.tt(cu[:, 1 - j, k:NT, :], cu[:, j, k:NT, :], cu[:, j, 0:NT - k, :], ALU.add)
            j = 1 - j
        cum = cu[:, j, :, :]
        g = self.ts(n8[:], cum[:, NT - 1, :], 127.0, None, ALU.add, None, f)
        g = V.do(lambda e: e.tensor_scalar(n8[:], n8[:], 7, None, ALU.arith_shift_right), g)
        g = nblk = self.copy_v(e8[:, 0, :], n8[:], g)
        i = 0
        for k in (1, 2, 4):
            self.copy_v(e8[:, i + 1, 0:k], e8[:, i, 0:k], g)
            g = self.tt(e8[:, i + 1, k:8], e8[:, i, k:8], e8[:, i, 0:8 - k], ALU.add)
            i += 1
        ends = e8[:, 3, :]
        s = self.tt(e8[:, 4, :], ends, e8[:, 0, :], ALU.subtract, g)
        s = self.ts(e8[:, 4, :], e8[:, 4, :], 128.0, None, ALU.mult, None, s)
        f = self.tt(pos[:], pre, cum, ALU.add, f)
        f = self.tt(pos[:], pos[:], tot, ALU.subtract, f)
        z.free = [f]
        f = self.tt(pos[:], pos[:], e8[:, 4, :].unsqueeze(1).to_broadcast([128, NT, 8]), ALU.add, f, s)
        last = f
        for k in range(2):
            q = self.tt(tm[:], oh[:, k, :, :], pos[:], ALU.mult, last)
            q = self.red(sm[:, 10, :], tm[:], ALU.add, q)
            last = self.copy_v(POS[:, k, :], sm[:, 10, :], q)
        placed = last
        for k in range(2):
            q = self.tt(tm[:], oh[:, k, :, :], esc[:].unsqueeze(1).to_broadcast([128, NT, 8]), ALU.mult, last, m3)
            q = self.red(sm[:, 11, :], tm[:], ALU.add, q)
            last = self.tt(sm[:, 6 + k, :], sm[:, 6 + k, :], sm[:, 11, :], ALU.mult, q, wts)
        wts = last
        r0 = lambda k: eb[:, k, :]
        g = self.tt(ge[:], jio[:].unsqueeze(2).to_broadcast([1, 40, 8]), ends[0:1, :].unsqueeze(1).to_broadcast([1, 40, 8]),
                    ALU.is_ge, g, consts, logits)
        g = self.red(r0(0), ge[:], ALU.add, g)
        g = self.ts(r0(0), r0(0), 7.0, None, ALU.min, None, g)
        a = V.do(lambda e: e.memset(r0(1)[:, 0:1], 0.0))
        b = V.do(lambda e: e.memset(r0(7), 0.0))
        g = self.tt(r0(1)[:, 1:40], r0(0)[:, 1:40], r0(0)[:, 0:39], ALU.not_equal, g)
        g = V.do(lambda e: e.tensor_tensor_scan(r0(2), r0(1), r0(7), 0.0, ALU.add, ALU.add), g, a, b)
        h = self.ts(r0(3), r0(2), 3.0, -3.0, ALU.is_ge, ALU.mult, g)
        h = self.ts(r0(4), r0(2), 6.0, -3.0, ALU.is_ge, ALU.mult, h)
        h = self.tt(r0(3), r0(3), r0(4), ALU.add, h)
        h = self.tt(r0(3), r0(3), r0(2), ALU.add, h)
        a = V.do(lambda e: e.memset(r0(1)[:, 0:1], 1.0), h)
        a = self.copy_v(EI[:, 0, :], r0(0), a)
        a = self.copy_v(EI[:, 1, :], r0(1), a)
        a = known = self.copy_v(EI[:, 2, :], r0(3), a)

        marks = []
        for t in range(NT):
            for k in range(2):
                m = self.ch("scatter").send(G, lambda e, t=t, k=k: e.indirect_dma_start(
                    self.XS, bass.IndirectOffsetOnAxis(POS[:, k, t:t + 1], 0), XN[:, t, :], None), placed, self.zeroed)
        scattered = m

        banks = self.banks
        R, reg = {}, {}

        def weights(j):
            SP.wait(known, R.get(("down", j - 3)), scattered if j == 2 else None)

            def f(e):
                ex = e.value_load(EI[0:1, 0, j:j + 1], min_val=0, max_val=7)
                ch = e.value_load(EI[0:1, 1, j:j + 1], min_val=0, max_val=1)
                bu = e.value_load(EI[0:1, 2, j:j + 1], min_val=0, max_val=2)
                return e.dma_start(WB[:, bass.ds(bu * 6144, 6144)], self.ins["moe_w"][bass.ds(ex * 128, 128), :], cond=ch)

            R["w", j] = self.ch(f"moew{j % 3}").send(SP, f)

        def rows(j):
            R["xs", j] = self.load(f"xs{j % 3}", xs[:, j % 3, :], self.XS[128 * j:128 * j + 128, :], scattered, R.get(("T", j - 3)))

        def turn(j):
            z = banks[j % 2]
            for c in range(4):
                m = self.transpose(z[:, 128 * c:128 * c + 128], xs[:, j % 3, 128 * c:128 * c + 128], R["xs", j], *z.free, mark=c == 3)
            R["T", j] = m
            f = self.copy_v(xsT[:, j % 2, :, :].rearrange("p c n -> p (c n)"), z[:], m, R.get(("up", j - 2)))
            z.free = [f]
            R["xt", j] = f

        def upper(j):
            PE.wait(known)

            def f(e):
                reg["b"] = e.value_load(EI[0:1, 2, j:j + 1], min_val=0, max_val=2)
            PE.ops.append(f)
            ms = []
            for half in range(2):
                z = banks[2 + half]
                PE.wait(R["xt", j], R["w", j], *z.free)
                for c in range(4):
                    o = 1024 * c + 512 * half
                    m = PE.do(lambda e, z=z, c=c, o=o: e.matmul(z[:], xsT[:, j % 2, c, :], WB[:, bass.ds(reg["b"] * 6144 + o, 512)],
                                                                start=c == 0, stop=c == 3), mark=c == 3)
                ms.append(m)
            R["up", j] = m
            f = self.act(gl[:], banks[2][:], ACT.Gelu_apprx_tanh, ms[0], R.get("gl"))
            banks[2].free = [f]
            f = self.tt(hh[:, j % 2, :], banks[3][:], gl[:], ALU.mult, f, ms[1], R.get(("Th", j - 2)))
            banks[3].free = [f]
            R["gl"] = f
            R["h", j] = f

        def mid(j):
            z = banks[4 + j % 2]
            for c in range(4):
                m = self.transpose(z[:, 128 * c:128 * c + 128], hh[:, j % 2, 128 * c:128 * c + 128], R["h", j], *z.free, mark=c == 3)
            R["Th", j] = m
            f = self.copy_v(hT[:, j % 2, :, :].rearrange("p c n -> p (c n)"), z[:], m, R.get(("down", j - 2)))
            z.free = [f]
            R["ht", j] = f

        def lower(j):
            z = banks[6 + j % 2]
            PE.wait(R["ht", j], *z.free)

            def f(e):
                reg["d"] = e.value_load(EI[0:1, 2, j:j + 1], min_val=0, max_val=2)
            PE.ops.append(f)
            for c in range(4):
                o = 4096 + 512 * c
                m = PE.do(lambda e, c=c, o=o: e.matmul(z[:], hT[:, j % 2, c, :], WB[:, bass.ds(reg["d"] * 6144 + o, 512)],
                                                       start=c == 0, stop=c == 3), mark=c == 3)
            R["down", j] = m
            f = self.copy_v(os_[:, j % 2, :], z[:], m, R.get(("out", j - 2)))
            z.free = [f]
            R["out", j] = self.load(f"os{j % 2}", self.OS[128 * j:128 * j + 128, :], os_[:, j % 2, :], f)

        acc = gt[:, 0:2, :, :].rearrange("p a k n -> p (a k) n")
        weights(0)
        weights(1)
        rows(0)
        rows(1)
        weights(2)
        rows(2)
        turn(0)
        upper(0)
        for j in range(NBLK):
            if j + 1 < NBLK:
                turn(j + 1)
            mid(j)
            if j + 1 < NBLK:
                upper(j + 1)
            lower(j)
            if j < 12:
                self.size(raw, j)
            elif j < 30 and j % 2:
                self.add_factor(raw, acc, j // 2 - 6)
            if j + 3 < NBLK:
                weights(j + 3)
                rows(j + 3)
        outs = [R["out", NBLK - 2], R["out", NBLK - 1], self.factors]

        def gather(t):
            for k in range(2):
                R["gt", t, k] = self.ch(f"gather{k}{t % 4}").send(G, lambda e, k=k: e.indirect_dma_start(
                    gt[:, t % 4, k, :], None, self.OS, bass.IndirectOffsetOnAxis(POS[:, k, t:t + 1], 0)), *outs, R.get(("g", t - 4)), s)

        for t in range(3):
            gather(t)
        for t in range(NT):
            if t + 3 < NT:
                gather(t + 3)
            x = self.X[:, t, :]
            for k in range(2):
                self.xtok[t] = self.stt(x, gt[:, t % 4, k, :], sm[:, 6 + k, t:t + 1], x, ALU.mult, ALU.add, R["gt", t, k], wts, self.xtok[t])
            R["g", t] = self.xtok[t]
            self.stat(t)
            if t == 0:
                self.early = self.ln_steps(plain=self.XF, each=True)
            else:
                next(self.early)

    def finish(self):
        self.fence()
        o = self.out.rearrange("b (t p) d -> p (b t) d", p=128)
        for h in range(4):
            m = self.load("out", o[:, 4 * h:4 * h + 4, :], self.X[:, 4 * h:4 * h + 4, :], *self.xtok[4 * h:4 * h + 4])
        self.SP.wait(m)

    def build(self):
        self.start()
        for p in self.phases:
            p(self)
        self.finish()
        with self.nc.Block() as block:
            block.tensor(self.PE.play)
            block.scalar(self.A.play)
            block.vector(self.V.play)
            block.gpsimd(self.G.play)
            block.sync(self.SP.play)


ALL = [lambda p: p.attend_wide(0), lambda p: p.experts(), lambda p: p.attend_l1(), lambda p: p.ternary_ffn(),
       lambda p: p.attend_l2(), lambda p: p.mix(), lambda p: p.attend_wide(3), lambda p: p.choice()]


def program(nc, ins, out, phases=ALL):
    Program(nc, ins, out, phases).build()


def lay_out(x):
    a = {k: np.asarray(v) for k, v in x.items()}

    def rows(w, n):
        return np.ascontiguousarray(w.reshape(n, 128, -1).transpose(1, 0, 2))

    out = {k: a[k] for k in ("x", "mask_BxS2_bf1", "fside_BxSx2_0", "L3_xattn_gq", "L3_xattn_gk",
                             "L0_ffn_per_expert_scale", "L3_ffn_router_b", "L3_ffn_expert_b",
                             "L1_xattn_bq", "L1_xattn_bk", "L1_xattn_bv", "L1_xattn_bkv_dca",
                             "L1_xattn_qn_w", "L1_xattn_qn_b", "L1_xattn_kn_w", "L1_xattn_kn_b",
                             "L1_xattn_kn_dca_w", "L1_xattn_kn_dca_b", "L1_xattn_bo", "L2_xattn_bout", "L2_ffn_bias")}
    out["mask_BxS2_bf1"] = a["mask_BxS2_bf1"].view(np.uint8)
    out["ctxT"] = rows(np.ascontiguousarray(a["ctx_1024"].reshape(T, C).T), 2)
    for L, kw in ((0, 128), (3, 256)):
        p = f"L{L}_xattn_"
        out[p + "Wq"] = a[p + "Wq"].reshape(4, 128, 8, 256).transpose(2, 1, 0, 3)
        for k in ("Wk", "Wv"):
            out[p + k] = a[p + k].reshape(2, 128, 8, kw).transpose(2, 1, 0, 3)
        out[p + "Wo"] = a[p + "Wo"].reshape(8, 2, 128, 512).transpose(0, 2, 1, 3)
    g = a["L0_ffn_gating_einsum"].transpose(0, 3, 1, 2).reshape(8, 4, 128, 1024).transpose(0, 2, 1, 3).reshape(8, 128, 4096)
    l = a["L0_ffn_linear"].reshape(8, 4, 128, 512).transpose(0, 2, 1, 3).reshape(8, 128, 2048)
    out["moe_w"] = np.concatenate([g, l], axis=2).reshape(8 * 128, 6144)
    out["L0_ffn_router_logits"] = rows(a["L0_ffn_router_logits"], 4)
    out["L0_ffn_router_scale"] = a["L0_ffn_router_scale"].reshape(4, 128).T
    out["L1_xattn_Wq"] = rows(a["L1_xattn_Wq"], 4)
    out["L1_xattn_Wkv"] = rows(np.concatenate([a["L1_xattn_Wk"], a["L1_xattn_Wv"]], axis=1), 2)
    out["L1_xattn_Wkv_dca"] = rows(a["L1_xattn_Wkv_dca"], 2)
    out["L1_xattn_Wo"] = rows(a["L1_xattn_Wo"], 4)
    out["ctx_dcaT"] = rows(np.ascontiguousarray(a["ctx_1024"][:, -16:, :].reshape(128, C).T), 2)
    for k in ("W_up", "W_gate"):
        out["L1_ffn_" + k] = a["L1_ffn_" + k].T.reshape(4, 128, 4, 512).transpose(2, 1, 0, 3)
    out["L1_ffn_W_down"] = a["L1_ffn_W_down"].T.reshape(4, 4, 128, 512).transpose(0, 2, 1, 3)
    out["L2_xattn_Wq"] = rows(a["L2_xattn_Wq"], 4)
    out["L2_xattn_Wkv"] = rows(a["L2_xattn_Wkv"], 2)
    out["L2_xattn_Wout"] = rows(a["L2_xattn_Wout"], 4)
    out["L2_ffn_factors"] = a["L2_ffn_factors"].reshape(8, 4, 128, 512).transpose(0, 2, 1, 3)
    out["L3_ffn_router_w"] = rows(a["L3_ffn_router_w"], 4)
    out["L3_ffn_expert_w"] = rows(a["L3_ffn_expert_w"], 4)
    return {k: np.ascontiguousarray(v) for k, v in out.items()}


def kernel(**inputs):
    import concourse.bacc as _bacc
    from concourse.bass_utils import run_bass_kernel_spmd as _run

    nc = _bacc.Bacc("TRN2", target_bir_lowering=False, num_devices=1)
    arrays = lay_out(inputs)
    ins = {k: nc.dram_tensor("in_" + k, v.shape, mybir.dt.from_np(v.dtype), kind="ExternalInput").ap() for k, v in arrays.items()}
    out = nc.dram_tensor("out_0", (NB, S, D), F32, kind="ExternalOutput").ap()
    program(nc, ins, out)
    r = _run(nc, [{"in_" + k: v for k, v in arrays.items()}], core_ids=[0])
    return r.results[0]["out_0"]
```
